# Optimizing a Trainium2 kernel written in Bass

```python
import numpy as np
import jax
import jax.numpy as jnp

def _softmax(x, axis=-1):
    return jax.nn.softmax(x, axis=axis)

def _gelu(x):
    return jax.nn.gelu(x, approximate=True)

def _silu(x):
    return jax.nn.silu(x)

def _sigmoid(x):
    return jax.nn.sigmoid(x)

def _layernorm(x, axis=-1, eps=1e-05):
    m = jnp.mean(x, axis=axis, keepdims=True)
    v = jnp.var(x, axis=axis, keepdims=True)
    return (x - m) / jnp.sqrt(v + eps)

def _scatter_add(tgt, idx, src, axis=0):
    return tgt.at[idx].add(src)

def _segment_sum(src, seg, n):
    return jax.ops.segment_sum(src, seg, n)
kernel_name = 'mk_gnn_preln_d4_gnn_r64_c4534a'

def setup_inputs(seed: int=0):
    np.random.seed(seed)
    _w = jnp.asarray

    def _rec_inputs():
        import jax
        import jax.numpy as jnp
        _gk = jax.random.key(seed)
        x = -0.0003713 + 1 * jax.random.normal(jax.random.fold_in(_gk, 1), (50000, 128), jnp.float32)
        src = jax.random.randint(jax.random.fold_in(_gk, 2), (25000,), 0, 50000, jnp.int32)
        dst = jax.random.randint(jax.random.fold_in(_gk, 3), (25000,), 0, 50000, jnp.int32)
        _o = jnp.argsort(dst, stable=True)
        src = src[_o]
        dst = dst[_o]
        edge_attr_128 = 5.93493e-05 + 1.00006 * jax.random.normal(jax.random.fold_in(_gk, 13), (25000, 128), jnp.float32)
        return (x, src, dst, edge_attr_128)
    x, src, dst, edge_attr_128 = _rec_inputs()

    def _L0_gnn_setup():
        import jax, jax.numpy as jnp
        import numpy as np
        N_NODES = 100000
        N_EDGES = 25000
        IN_CH = 128
        HID_CH = 128
        NEG_SLOPE = 0.01
        key = jax.random.key(seed)
        ks = jax.random.split(key, 8)
        scale_in = 1.0 / np.sqrt(IN_CH)
        scale_h = 1.0 / np.sqrt(HID_CH)
        return {'x': jax.random.normal(ks[0], (N_NODES, IN_CH), dtype=jnp.float32), 'edge_index': jax.random.randint(ks[1], (2, N_EDGES), 0, N_NODES, dtype=jnp.int64), 'Wl1': jax.random.normal(ks[2], (HID_CH, IN_CH), dtype=jnp.float32) * scale_in, 'bl1': jnp.zeros((HID_CH,), dtype=jnp.float32), 'Wr1': jax.random.normal(ks[3], (HID_CH, IN_CH), dtype=jnp.float32) * scale_in, 'Wlh': jax.random.normal(ks[4], (2, HID_CH, HID_CH), dtype=jnp.float32) * scale_h, 'blh': jnp.zeros((2, HID_CH), dtype=jnp.float32), 'Wrh': jax.random.normal(ks[5], (2, HID_CH, HID_CH), dtype=jnp.float32) * scale_h}
    _L0_gnn_all = _L0_gnn_setup()
    _L0_gnn_in = {k: v for k, v in _L0_gnn_all.items() if k in ('Wl1', 'bl1', 'Wr1', 'Wlh', 'blh', 'Wrh')}
    del _L0_gnn_all

    def _L1_gnn_setup():
        import jax, jax.numpy as jnp
        import numpy as np
        N = 100000
        E = 25000
        D = 128
        H = 128

        def _gcn_norm(edge_index, n):
            loop = jnp.arange(n, dtype=edge_index.dtype)
            src = jnp.concatenate([edge_index[0], loop])
            dst = jnp.concatenate([edge_index[1], loop])
            deg = jax.ops.segment_sum(jnp.ones_like(src, dtype=jnp.float32), dst, num_segments=n)
            dinv = jnp.where(deg > 0, jax.lax.rsqrt(deg), 0.0)
            norm = dinv[src] * dinv[dst]
            return (src, dst, norm)

        def _gcn_layer(x, W, b, src, dst, norm, n):
            h = x @ W
            msg = h[src] * norm[:, None]
            out = jax.ops.segment_sum(msg, dst, num_segments=n)
            return out + b
        key = jax.random.key(seed)
        ks = jax.random.split(key, 10)

        def lin_w(k, fan_in, fan_out):
            return jax.random.normal(k, (fan_in, fan_out), jnp.float32) / np.float32(np.sqrt(fan_in))
        x = jax.random.normal(ks[0], (N, D), jnp.float32)
        edge_index = jax.random.randint(ks[1], (2, E), 0, N)
        return {'x': x, 'edge_index': edge_index, 'W0': lin_w(ks[2], D, H), 'b0': jnp.zeros((H,), jnp.float32), 'W1': lin_w(ks[3], H, H), 'b1': jnp.zeros((H,), jnp.float32), 'W2': lin_w(ks[4], H, H), 'b2': jnp.zeros((H,), jnp.float32), 'Wr': lin_w(ks[5], D, H), 'br': jnp.zeros((H,), jnp.float32)}
    _L1_gnn_all = _L1_gnn_setup()
    _L1_gnn_in = {k: v for k, v in _L1_gnn_all.items() if k in ('W0', 'b0', 'W1', 'b1', 'W2', 'b2', 'Wr', 'br')}
    del _L1_gnn_all

    def _L2_gnn_setup():
        import jax, jax.numpy as jnp
        import numpy as np
        N_NODES = 100000
        N_EDGES = 9375
        D = 128
        HID = 512
        N_GRAPHS = 16
        MLP_IN = D + 3 * D + 1
        key = jax.random.key(seed)
        ks = jax.random.split(key, 9)
        x = jax.random.normal(ks[0], (N_NODES, D), dtype=jnp.float32)
        edge_index = jax.random.randint(ks[1], (2, N_EDGES), 0, N_NODES, dtype=jnp.int64)
        edge_attr = jax.random.normal(ks[2], (N_EDGES, D), dtype=jnp.float32)
        u = jax.random.normal(ks[3], (N_GRAPHS, 1), dtype=jnp.float32)
        batch = jnp.sort(jax.random.randint(ks[4], (N_NODES,), 0, N_GRAPHS, dtype=jnp.int64))
        s1 = 1.0 / np.sqrt(MLP_IN)
        s2 = 1.0 / np.sqrt(HID)
        W1 = jax.random.uniform(ks[5], (MLP_IN, HID), jnp.float32, -s1, s1)
        b1 = jax.random.uniform(ks[6], (HID,), jnp.float32, -s1, s1)
        W2 = jax.random.uniform(ks[7], (HID, D), jnp.float32, -s2, s2)
        b2 = jax.random.uniform(ks[8], (D,), jnp.float32, -s2, s2)
        return {'x': x, 'edge_index': edge_index, 'edge_attr': edge_attr, 'u': u, 'batch': batch, 'W1': W1, 'b1': b1, 'W2': W2, 'b2': b2}
    _L2_gnn_all = _L2_gnn_setup()
    _L2_gnn_in = {k: v for k, v in _L2_gnn_all.items() if k in ('u', 'W1', 'b1', 'W2', 'b2')}
    del _L2_gnn_all

    def _L3_gnn_setup():
        import jax, jax.numpy as jnp
        import numpy as np
        N_NODES = 100000
        N_EDGES = 25000
        D = 128
        H = 8
        DH = D // H
        DFF = 2 * D
        EPS_LN = 1e-05

        def _ln(x, g, b):
            mu = jnp.mean(x, axis=-1, keepdims=True)
            var = jnp.var(x, axis=-1, keepdims=True)
            return (x - mu) * jax.lax.rsqrt(var + EPS_LN) * g + b
        key = jax.random.key(seed)
        ks = jax.random.split(key, 12)
        s = 1.0 / np.sqrt(D)
        inp = {'h': jax.random.normal(ks[0], (N_NODES, D), jnp.float32), 'src': jax.random.randint(ks[1], (N_EDGES,), 0, N_NODES, jnp.int32), 'dst': jax.random.randint(ks[2], (N_EDGES,), 0, N_NODES, jnp.int32), 'Wq': jax.random.normal(ks[3], (D, D), jnp.float32) * s, 'Wk': jax.random.normal(ks[4], (D, D), jnp.float32) * s, 'Wv': jax.random.normal(ks[5], (D, D), jnp.float32) * s, 'Wo': jax.random.normal(ks[6], (D, D), jnp.float32) * s, 'bo': jnp.zeros((D,), jnp.float32), 'ln1_g': jnp.ones((D,), jnp.float32), 'ln1_b': jnp.zeros((D,), jnp.float32), 'W1': jax.random.normal(ks[7], (D, DFF), jnp.float32) * s, 'b1': jnp.zeros((DFF,), jnp.float32), 'W2': jax.random.normal(ks[8], (DFF, D), jnp.float32) * (1.0 / np.sqrt(DFF)), 'b2': jnp.zeros((D,), jnp.float32), 'ln2_g': jnp.ones((D,), jnp.float32), 'ln2_b': jnp.zeros((D,), jnp.float32)}
        return inp
    _L3_gnn_all = _L3_gnn_setup()
    _L3_gnn_in = {k: v for k, v in _L3_gnn_all.items() if k in ('Wq', 'Wk', 'Wv', 'Wo', 'bo', 'ln1_g', 'ln1_b', 'W1', 'b1', 'W2', 'b2', 'ln2_g', 'ln2_b')}
    del _L3_gnn_all
    return {'x': x, 'src': src, 'dst': dst, 'edge_attr_128': edge_attr_128, 'L0_gnn_Wl1': _L0_gnn_in['Wl1'], 'L0_gnn_bl1': _L0_gnn_in['bl1'], 'L0_gnn_Wr1': _L0_gnn_in['Wr1'], 'L0_gnn_Wlh': _L0_gnn_in['Wlh'], 'L0_gnn_blh': _L0_gnn_in['blh'], 'L0_gnn_Wrh': _L0_gnn_in['Wrh'], 'L1_gnn_W0': _L1_gnn_in['W0'], 'L1_gnn_b0': _L1_gnn_in['b0'], 'L1_gnn_W1': _L1_gnn_in['W1'], 'L1_gnn_b1': _L1_gnn_in['b1'], 'L1_gnn_W2': _L1_gnn_in['W2'], 'L1_gnn_b2': _L1_gnn_in['b2'], 'L1_gnn_Wr': _L1_gnn_in['Wr'], 'L1_gnn_br': _L1_gnn_in['br'], 'L2_gnn_u': _L2_gnn_in['u'], 'L2_gnn_W1': _L2_gnn_in['W1'], 'L2_gnn_b1': _L2_gnn_in['b1'], 'L2_gnn_W2': _L2_gnn_in['W2'], 'L2_gnn_b2': _L2_gnn_in['b2'], 'L3_gnn_Wq': _L3_gnn_in['Wq'], 'L3_gnn_Wk': _L3_gnn_in['Wk'], 'L3_gnn_Wv': _L3_gnn_in['Wv'], 'L3_gnn_Wo': _L3_gnn_in['Wo'], 'L3_gnn_bo': _L3_gnn_in['bo'], 'L3_gnn_ln1_g': _L3_gnn_in['ln1_g'], 'L3_gnn_ln1_b': _L3_gnn_in['ln1_b'], 'L3_gnn_W1': _L3_gnn_in['W1'], 'L3_gnn_b1': _L3_gnn_in['b1'], 'L3_gnn_W2': _L3_gnn_in['W2'], 'L3_gnn_b2': _L3_gnn_in['b2'], 'L3_gnn_ln2_g': _L3_gnn_in['ln2_g'], 'L3_gnn_ln2_b': _L3_gnn_in['ln2_b']}

def reference(x, src, dst, edge_attr_128, L0_gnn_Wl1, L0_gnn_bl1, L0_gnn_Wr1, L0_gnn_Wlh, L0_gnn_blh, L0_gnn_Wrh, L1_gnn_W0, L1_gnn_b0, L1_gnn_W1, L1_gnn_b1, L1_gnn_W2, L1_gnn_b2, L1_gnn_Wr, L1_gnn_br, L2_gnn_u, L2_gnn_W1, L2_gnn_b1, L2_gnn_W2, L2_gnn_b2, L3_gnn_Wq, L3_gnn_Wk, L3_gnn_Wv, L3_gnn_Wo, L3_gnn_bo, L3_gnn_ln1_g, L3_gnn_ln1_b, L3_gnn_W1, L3_gnn_b1, L3_gnn_W2, L3_gnn_b2, L3_gnn_ln2_g, L3_gnn_ln2_b):
    import jax
    import jax.numpy as jnp

    def _L0_gnn_ref(x, edge_index, Wl1, bl1, Wr1, Wlh, blh, Wrh):
        import jax, jax.numpy as jnp
        import numpy as np
        N_NODES = 100000
        N_EDGES = 25000
        IN_CH = 128
        HID_CH = 128
        NEG_SLOPE = 0.01
        N = x.shape[0]
        src = edge_index[0]
        dst = edge_index[1]
        deg = jax.ops.segment_sum(jnp.ones_like(dst, dtype=x.dtype), dst, num_segments=N)
        inv_deg = (1.0 / jnp.maximum(deg, 1.0))[:, None]

        def sage_conv(h, Wl, b, Wr):
            agg = jax.ops.segment_sum(h[src], dst, num_segments=N) * inv_deg
            return agg @ Wl.T + b + h @ Wr.T
        h = jax.nn.leaky_relu(sage_conv(x, Wl1, bl1, Wr1), NEG_SLOPE)
        for i in range(Wlh.shape[0]):
            h = jax.nn.leaky_relu(sage_conv(h, Wlh[i], blh[i], Wrh[i]), NEG_SLOPE)
        return h

    def _L1_gnn_ref(x, edge_index, W0, b0, W1, b1, W2, b2, Wr, br):
        import jax, jax.numpy as jnp
        import numpy as np
        N = 100000
        E = 25000
        D = 128
        H = 128

        def _gcn_norm(edge_index, n):
            loop = jnp.arange(n, dtype=edge_index.dtype)
            src = jnp.concatenate([edge_index[0], loop])
            dst = jnp.concatenate([edge_index[1], loop])
            deg = jax.ops.segment_sum(jnp.ones_like(src, dtype=jnp.float32), dst, num_segments=n)
            dinv = jnp.where(deg > 0, jax.lax.rsqrt(deg), 0.0)
            norm = dinv[src] * dinv[dst]
            return (src, dst, norm)

        def _gcn_layer(x, W, b, src, dst, norm, n):
            h = x @ W
            msg = h[src] * norm[:, None]
            out = jax.ops.segment_sum(msg, dst, num_segments=n)
            return out + b
        n = x.shape[0]
        src, dst, norm = _gcn_norm(edge_index, n)
        residual = x @ Wr + br
        h = jax.nn.relu(_gcn_layer(x, W0, b0, src, dst, norm, n)) + residual
        h = jax.nn.relu(_gcn_layer(h, W1, b1, src, dst, norm, n))
        h = jax.nn.relu(_gcn_layer(h, W2, b2, src, dst, norm, n))
        return h

    def _L2_gnn_ref(x, edge_index, edge_attr, u, batch, W1, b1, W2, b2):
        import jax, jax.numpy as jnp
        import numpy as np
        N_NODES = 100000
        N_EDGES = 9375
        D = 128
        HID = 512
        N_GRAPHS = 16
        MLP_IN = D + 3 * D + 1
        N = x.shape[0]
        row = edge_index[0]
        ones = jnp.ones((edge_attr.shape[0], 1), dtype=edge_attr.dtype)
        cnt = jax.ops.segment_sum(ones, row, num_segments=N)
        agg_sum = jax.ops.segment_sum(edge_attr, row, num_segments=N)
        agg_max = jax.ops.segment_max(edge_attr, row, num_segments=N)
        agg_max = jnp.where(cnt > 0, agg_max, jnp.zeros((), edge_attr.dtype))
        agg_mean = agg_sum / jnp.maximum(cnt, 1.0)
        h = jnp.concatenate([x, agg_sum, agg_max, agg_mean, u[batch]], axis=1)
        h = jax.nn.relu(h @ W1 + b1) @ W2 + b2
        return h + x

    def _L3_gnn_ref(h, src, dst, Wq, Wk, Wv, Wo, bo, ln1_g, ln1_b, W1, b1, W2, b2, ln2_g, ln2_b):
        import jax, jax.numpy as jnp
        import numpy as np
        N_NODES = 100000
        N_EDGES = 25000
        D = 128
        H = 8
        DH = D // H
        DFF = 2 * D
        EPS_LN = 1e-05

        def _ln(x, g, b):
            mu = jnp.mean(x, axis=-1, keepdims=True)
            var = jnp.var(x, axis=-1, keepdims=True)
            return (x - mu) * jax.lax.rsqrt(var + EPS_LN) * g + b
        n = h.shape[0]
        Q = (h @ Wq).reshape(n, H, DH)
        K = (h @ Wk).reshape(n, H, DH)
        V = (h @ Wv).reshape(n, H, DH)
        score = jnp.einsum('ehd,ehd->eh', K[src], Q[dst]) / np.sqrt(DH)
        score = jnp.exp(jnp.clip(score, -5.0, 5.0))
        m = V[src] * score[:, :, None]
        wV = jax.ops.segment_sum(m, dst, num_segments=n)
        z = jax.ops.segment_sum(score, dst, num_segments=n)
        h_attn = (wV / (z[:, :, None] + 1e-06)).reshape(n, D)
        x = h + (h_attn @ Wo + bo)
        x = _ln(x, ln1_g, ln1_b)
        y = jax.nn.relu(x @ W1 + b1) @ W2 + b2
        x = _ln(x + y, ln2_g, ln2_b)
        return x
    edge_index = jnp.stack([src, dst])
    batch0 = jnp.zeros((50000,), jnp.int32)
    h = jnp.maximum(_layernorm(x, axis=-1), 0.0)
    x = x + _L0_gnn_ref(h, edge_index, L0_gnn_Wl1, L0_gnn_bl1, L0_gnn_Wr1, L0_gnn_Wlh, L0_gnn_blh, L0_gnn_Wrh)
    h = jnp.maximum(_layernorm(x, axis=-1), 0.0)
    x = x + _L1_gnn_ref(h, edge_index, L1_gnn_W0, L1_gnn_b0, L1_gnn_W1, L1_gnn_b1, L1_gnn_W2, L1_gnn_b2, L1_gnn_Wr, L1_gnn_br)
    h = jnp.maximum(_layernorm(x, axis=-1), 0.0)
    x = x + _L2_gnn_ref(h, edge_index, edge_attr_128, L2_gnn_u, batch0, L2_gnn_W1, L2_gnn_b1, L2_gnn_W2, L2_gnn_b2)
    h = jnp.maximum(_layernorm(x, axis=-1), 0.0)
    x = x + _L3_gnn_ref(h, src, dst, L3_gnn_Wq, L3_gnn_Wk, L3_gnn_Wv, L3_gnn_Wo, L3_gnn_bo, L3_gnn_ln1_g, L3_gnn_ln1_b, L3_gnn_W1, L3_gnn_b1, L3_gnn_W2, L3_gnn_b2, L3_gnn_ln2_g, L3_gnn_ln2_b)
    return x

_drawn_inputs = setup_inputs


def setup_inputs(seed=0):
    import zlib

    import numpy as np

    out = dict(_drawn_inputs(seed))
    spreads = {'L0_gnn_bl1': (0.0, 0.1),
     'L0_gnn_blh': (0.0, 0.1),
     'L1_gnn_b0': (0.0, 0.1),
     'L1_gnn_b1': (0.0, 0.1),
     'L1_gnn_b2': (0.0, 0.1),
     'L1_gnn_br': (0.0, 0.1),
     'L3_gnn_bo': (0.0, 0.1),
     'L3_gnn_ln1_g': (1.0, 0.2),
     'L3_gnn_ln1_b': (0.0, 0.1),
     'L3_gnn_b1': (0.0, 0.361),
     'L3_gnn_b2': (0.0, 0.269),
     'L3_gnn_ln2_g': (1.0, 0.2),
     'L3_gnn_ln2_b': (0.0, 0.1)}
    factors = {'L2_gnn_u': 8.0,
     'L2_gnn_b1': 8.0,
     'L2_gnn_b2': 4.014,
     'L3_gnn_Wq': 3.14,
     'L3_gnn_Wk': 3.164}
    for name, (base, spread) in spreads.items():
        noise = np.random.default_rng([zlib.crc32(name.encode()), seed]).standard_normal(out[name].shape)
        drawn = base * np.exp(spread * noise) if base else spread * noise
        out[name] = jnp.asarray(drawn.astype(out[name].dtype))
    for name, factor in factors.items():
        out[name] = (out[name] * factor).astype(out[name].dtype)
    return out
```

```python
from contextlib import ExitStack

import concourse.bass as bass
from concourse import mybir

P = 128
D = 128
N = 50000
SUB = 4
BLK = P * SUB
NB = -(-N // BLK)
NB += NB % 2
NPAD = NB * BLK
TAILP = (N - (NB - 1) * BLK) // SUB
assert TAILP * SUB + (NB - 1) * BLK == N and 0 < TAILP <= P
E = 25000
EC = 125
NC = E // EC
assert NC * EC == E
NCOL = NB * SUB
HALF = NC // 2
H = 8
DH = D // H
HID = 512
HG = HID // P
DFF = 256
FG = DFF // P
EPS = 1e-5
LEAK = 0.01
SKIP = float(NPAD + 1)
NEG = -3.0e38

F32 = mybir.dt.float32
BF16 = mybir.dt.bfloat16
I32 = mybir.dt.int32
ALU = mybir.AluOpType
ACT = mybir.ActivationFunctionType
AX = mybir.AxisListType


def blocks(ap):
    return ap.rearrange("(b p k) d -> b p k d", p=P, k=SUB)


def wait(eng, sem, value):
    if isinstance(value, int) and value <= 0:
        return
    eng.wait_ge(sem, value)


def alone(eng, sem, value, least=1):
    if not isinstance(value, int):
        eng.wait_ge(sem, least)
    wait(eng, sem, value)


def steps(eng, stages, total, unroll, head, tail):
    last = max(lag for lag, _ in stages)

    def step(s):
        for lag, f in stages:
            if 0 <= s - lag < total:
                f(s - lag, (s - lag) % unroll, (s - lag) // unroll)

    assert head % unroll == 0 and head >= last and (total - tail) % unroll == 0
    for s in range(head):
        step(s)
    with eng.Fori(head // unroll, (total - tail) // unroll) as j:
        for v in range(unroll):
            for lag, f in stages:
                u, back = (v - lag) % unroll, (v - lag) // unroll
                q = j + back if back else j
                f(q * unroll + u, u, q)
    for s in range(total - tail, total + last):
        step(s)


class Phase:

    def __init__(self, nc, name):
        self.nc, self.name = nc, name
        self.stack = ExitStack()
        self.sems = []

    def sb(self, name, shape, dt=F32):
        return self.stack.enter_context(self.nc.sbuf_tensor(f"{self.name}_{name}", shape, dt))

    def ps(self, name, shape, dt=F32):
        return self.stack.enter_context(self.nc.psum_tensor(f"{self.name}_{name}", shape, dt))

    def sem(self, name):
        s = self.nc.alloc_semaphore(name=f"{self.name}_{name}")
        self.sems.append(s)
        return s

    def __enter__(self):
        return self

    def __exit__(self, kind, value, trace):
        if kind is None:
            self.nc.clear_and_free_semaphores(self.sems)
            self.nc.all_engine_barrier()
        self.stack.__exit__(kind, value, trace)


class Chain:

    def __init__(self, eng, sem, per):
        self.eng, self.sem, self.per = eng, sem, per

    def start(self, item):
        self.base, self.made = item * self.per, 0

    def link(self, ins):
        self.made += 1
        ins.then_inc(self.sem, 1)
        self.eng.wait_ge(self.sem, self.base + self.made)

    def end(self):
        assert self.made == self.per, (self.made, self.per)


def constants(nc, k):
    with Phase(nc, "const") as ph:
        ones = ph.sb("ones", [P, P])
        zero = ph.sb("zero", [P, SUB * 2 * D])
        made, z = ph.sem("made"), ph.sem("zeroed")
        agg = k["AGG"].rearrange("(p m) d -> p (m d)", p=P)
        agg2 = k["AGG2"].rearrange("(p m) d -> p (m d)", p=P)
        width = SUB * 2 * D
        with nc.Block() as block:
            @block.gpsimd
            def _(pool):
                nc.gpsimd.memset(ones[:, :], 1.0).then_inc(made, 1)
                pool.wait_ge(made, 1)
                nc.gpsimd.affine_select(out=k["ident"][:, :], in_=ones[:, :], compare_op=ALU.is_equal,
                                        fill=0.0, base=0, pattern=[[-1, P]], channel_multiplier=1)
                nc.gpsimd.affine_select(out=k["before"][:, :], in_=ones[:, :], compare_op=ALU.is_gt,
                                        fill=0.0, base=0, pattern=[[-1, P]], channel_multiplier=1)
                nc.gpsimd.affine_select(out=k["upper"][:, :], in_=ones[:, :], compare_op=ALU.is_gt,
                                        fill=0.0, base=0, pattern=[[1, P]], channel_multiplier=-1)
                nc.gpsimd.affine_select(out=k["lastrow"][:, :], in_=ones[:, 0:1], compare_op=ALU.is_equal,
                                        fill=0.0, base=-(EC - 1), pattern=[[1, 1]], channel_multiplier=1)
                nc.gpsimd.iota(k["count"][:, :], pattern=[[1, NCOL]], base=0, channel_multiplier=0,
                               allow_small_or_imprecise_dtypes=True)
                nc.gpsimd.memset(k["eps"][:, :], EPS)
                nc.gpsimd.memset(k["half"][:, :], -0.5).then_inc(made, 1)

            @block.vector
            def _(dve):
                nc.vector.memset(zero[:, :], 0.0).then_inc(z, 1)
                dve.wait_ge(made, 2)
                nc.vector.tensor_copy(k["identb"][:, :], k["ident"][:, :])
                nc.vector.memset(k["one"][:, :], 1.0)

            @block.sync
            def _(sp):
                sp.wait_ge(z, 1)
                n1 = NPAD // P * D // width
                n2 = NPAD // P * 2 * D // width
                stored = ph.sem("stored")
                with sp.Fori(0, n1) as i:
                    sp.dma_start(agg[:, bass.ts(i, width)], zero[:, :]).then_inc(stored, 16)
                with sp.Fori(0, n2) as i:
                    sp.dma_start(agg2[:, bass.ts(i, width)], zero[:, :]).then_inc(stored, 16)
                assert n1 * width * P == NPAD * D
                sp.wait_ge(stored, 16 * (n1 + n2))


def sort_edges(nc, k, name, key, other, SRT, deg, keys_dram, keyrow, t):
    rows = lambda ap: ap.rearrange("(a c p) -> c a p", a=2, p=EC)
    with Phase(nc, name) as ph:
        keycol = ph.sb("keycol", [EC, NC])
        keyint = ph.sb("keyint", [EC, NC], I32)
        lo = ph.sb("lo", [EC, NC])
        hi = ph.sb("hi", [EC, NC])
        part = ph.sb("part", [EC, 3, NC], I32)
        rec = ph.sb("rec", [EC, NC, 2], I32)
        where = ph.sb("where", [EC, NC], I32)
        with Phase(nc, name + "h") as h:
            raw = h.sb("raw", [HALF, 2, 2, EC], I32)
            rawf = h.sb("rawf", [HALF, 2, 2, EC])
            ohlo = h.sb("ohlo", [EC, 2, P], BF16)
            ohhi = h.sb("ohhi", [EC, 2, NCOL], BF16)
            run = h.sb("run", [P, NCOL])
            rowoff = h.sb("rowoff", [P, 1])
            tp = h.ps("tp", [P, 512])
            hist = h.ps("hist", [P, 512])
            off = h.ps("off", [P, 512])
            loaded, conv, turned, cols, oh, counted, chain, offed = (
                h.sem(x) for x in ("loaded", "conv", "turned", "cols", "oh", "counted", "chain", "offed"))
            nload = 2 if other is not None else 1
            with nc.Block() as block:
                @block.sync
                def _(sp):
                    sp.dma_start(raw[:, 0, :, :], rows(key)).then_inc(loaded, 16)
                    if other is not None:
                        sp.dma_start(raw[:, 1, :, :], rows(other)).then_inc(loaded, 16)
                    sp.dma_start(keyrow[:, 1:1 + E],
                                 key.rearrange("(a e) -> a e", a=1).broadcast_to([P, E])).then_inc(loaded, 16)
                    sp.wait_ge(loaded, 16 * (nload + 1))

                @block.gpsimd
                def _(pool):
                    if other is None:
                        nc.gpsimd.iota(rec[:, :, 1], pattern=[[EC, NC]], base=0, channel_multiplier=1)

                @block.vector
                def _(dve):
                    ch = Chain(dve, chain, 7 if other is None else 7)
                    ch.start(0)
                    dve.wait_ge(loaded, 16 * (nload + 1))
                    for x in range(nload):
                        last = nc.vector.tensor_copy(rawf[:, x, :, :], raw[:, x, :, :])
                    last.then_inc(conv, 1)
                    dve.wait_ge(turned, 1)
                    ch.link(nc.vector.tensor_copy(keycol[:, :], tp[0:EC, 0:NC]))
                    if other is not None:
                        nc.vector.tensor_copy(rec[:, :, 1], tp[0:EC, NC:2 * NC])
                    nc.vector.tensor_copy(rec[:, :, 0], keycol[:, :])
                    ch.link(nc.vector.tensor_copy(keyint[:, :], keycol[:, :]))
                    nc.vector.tensor_scalar(part[:, 0, :], keyint[:, :], 2, P - 1,
                                            ALU.logical_shift_right, ALU.bitwise_and)
                    nc.vector.tensor_scalar(part[:, 1, :], keyint[:, :], 9, None, ALU.logical_shift_right)
                    ch.link(nc.vector.tensor_scalar(part[:, 2, :], keyint[:, :], 3, None, ALU.bitwise_and))
                    nc.vector.tensor_copy(lo[:, :], part[:, 0, :])
                    ch.link(nc.vector.scalar_tensor_tensor(hi[:, :], part[:, 1, :], 4.0, part[:, 2, :],
                                                           ALU.mult, ALU.add))

                    def onehots(c, u, q):
                        wait(dve, counted, c - 1)
                        nc.vector.tensor_scalar(ohlo[:, u, :], k["count"][0:EC, 0:P], lo[:, bass.ds(c, 1)],
                                                None, ALU.is_equal)
                        nc.vector.tensor_scalar(ohhi[:, u, :], k["count"][0:EC, :], hi[:, bass.ds(c, 1)],
                                                None, ALU.is_equal).then_inc(oh, 1)
                    steps(dve, [(0, onehots)], NC, 2, 2, 2)
                    dve.wait_ge(counted, NC)
                    ch.link(nc.vector.tensor_copy(deg[:, :], hist[:, 0:NCOL]))
                    nc.vector.tensor_tensor_scan(run[:, :], k["one"][:, :], deg[:, :], 0.0, ALU.mult,
                                                 ALU.add).then_inc(chain, 1)
                    ch.made += 1
                    dve.wait_ge(offed, 1)
                    ch.link(nc.vector.tensor_copy(rowoff[:, :], off[:, 0:1]))
                    nc.vector.scalar_tensor_tensor(k["start"][:, :], run[:, :], rowoff[:, :], deg[:, :],
                                                   ALU.add, ALU.subtract)
                    ch.end()

                @block.tensor
                def _(pe):
                    pe.wait_ge(conv, 1)
                    for x in range(nload):
                        for a in range(2):
                            last = nc.tensor.transpose(tp[0:EC, (2 * x + a) * HALF:(2 * x + a + 1) * HALF],
                                                       rawf[:, x, a, :], k["ident"][0:HALF, 0:HALF])
                    last.then_inc(turned, 1)

                    def count(c, u, q):
                        pe.wait_ge(oh, c + 1)
                        nc.tensor.matmul(hist[:, 0:NCOL], ohlo[:, u, :], ohhi[:, u, :],
                                         start=isinstance(c, int) and c == 0,
                                         stop=isinstance(c, int) and c == NC - 1).then_inc(counted, 1)
                    steps(pe, [(0, count)], NC, 2, 2, 2)
                    pe.wait_ge(chain, 6)
                    nc.tensor.matmul(off[:, 0:1], k["upper"][:, :], run[:, NCOL - 1:NCOL],
                                     start=True, stop=True).then_inc(offed, 1)

        with Phase(nc, name + "r") as r:
            ohlo = r.sb("ohlo", [EC, 2, P], BF16)
            ohhi = r.sb("ohhi", [EC, 2, NCOL], BF16)
            lot = r.sb("lot", [P, 2, EC])
            tbl = r.sb("tbl", [P, 2, NCOL])
            junk = r.sb("junk", [EC, 2, NCOL])
            junk2 = r.sb("junk2", [EC, 2, EC])
            base = r.sb("base", [EC, NC])
            inner = r.sb("inner", [EC, NC])
            psT = [r.ps(f"psT{u}", [P, 1024], BF16) for u in range(2)]
            psU = [r.ps(f"psU{u}", [P, 512]) for u in range(2)]
            psL = [r.ps(f"psL{u}", [P, 512]) for u in range(2)]
            oh, added, lotted, table, looked, dotted, first, placed, chain = (
                r.sem(x) for x in ("oh", "added", "lotted", "table", "looked", "dotted", "first",
                                   "placed", "chain"))
            with nc.Block() as block:
                @block.vector
                def _(dve):
                    nc.vector.tensor_copy(tbl[:, 0, :], k["start"][:, :]).then_inc(first, 1)
                    dve.wait_ge(first, 1)

                    def onehots(c, u, q):
                        wait(dve, added, c - 1)
                        nc.vector.tensor_scalar(ohlo[:, u, :], k["count"][0:EC, 0:P], lo[:, bass.ds(c, 1)],
                                                None, ALU.is_equal)
                        nc.vector.tensor_scalar(ohhi[:, u, :], k["count"][0:EC, :], hi[:, bass.ds(c, 1)],
                                                None, ALU.is_equal).then_inc(oh, 1)

                    def advance(c, u, q):
                        dve.wait_ge(added, c + 1)
                        wait(dve, looked, c)
                        wait(dve, table, c)
                        nc.vector.tensor_tensor(tbl[:, 1 - u, :], tbl[:, u, :], psU[u][:, 0:NCOL],
                                                ALU.add).then_inc(table, 1)

                    def pick(c, u, q):
                        dve.wait_ge(looked, c + 1)
                        wait(dve, dotted, c - 1)
                        nc.vector.scalar_tensor_tensor(junk[:, u, :], k["count"][0:EC, :],
                                                       hi[:, bass.ds(c, 1)], psL[u][0:EC, 0:NCOL],
                                                       ALU.is_equal, ALU.mult,
                                                       accum_out=base[:, bass.ds(c, 1)])
                        nc.vector.scalar_tensor_tensor(junk2[:, u, :], keyrow[0:EC, bass.ds(c * EC + 1, EC)],
                                                       keycol[:, bass.ds(c, 1)], k["before"][0:EC, 0:EC],
                                                       ALU.is_equal, ALU.mult,
                                                       accum_out=inner[:, bass.ds(c, 1)]).then_inc(dotted, 1)
                    steps(dve, [(0, onehots), (1, advance), (2, pick)], NC, 2, 4, 2)
                    dve.wait_ge(dotted, NC)
                    nc.vector.scalar_tensor_tensor(where[:, :], base[:, :], 1.0, inner[:, :], ALU.add,
                                                   ALU.add).then_inc(placed, 1)

                @block.scalar
                def _(act):
                    def turn(c, u, q):
                        act.wait_ge(added, c + 1)
                        wait(act, looked, c - 1)
                        nc.scalar.activation(lot[:, u, :], psT[u][:, 0:EC], ACT.Copy).then_inc(lotted, 1)
                    steps(act, [(0, turn)], NC, 2, 2, 2)

                @block.tensor
                def _(pe):
                    def spread(c, u, q):
                        pe.wait_ge(oh, c + 1)
                        wait(pe, lotted, c - 1)
                        wait(pe, table, c - 1)
                        nc.tensor.transpose(psT[u][:, 0:EC], ohlo[:, u, :], k["identb"][0:EC, 0:EC])
                        nc.tensor.matmul(psU[u][:, 0:NCOL], ohlo[:, u, :], ohhi[:, u, :], start=True,
                                         stop=True).then_inc(added, 1)

                    def look(c, u, q):
                        pe.wait_ge(lotted, c + 1)
                        wait(pe, table, c)
                        if isinstance(c, int) and c == 0:
                            pe.wait_ge(first, 1)
                        wait(pe, dotted, c - 1)
                        nc.tensor.matmul(psL[u][0:EC, 0:NCOL], lot[:, u, :], tbl[:, u, :], start=True,
                                         stop=True).then_inc(looked, 1)
                    steps(pe, [(0, spread), (1, look)], NC, 2, 4, 2)

                @block.gpsimd
                def _(pool):
                    minus = r.sb("minus", [2, 2], I32)
                    sent = r.sem("sent")
                    ring = [r.sem(f"ring{i}") for i in range(4)]
                    nc.gpsimd.memset(minus[:, :], -1).then_inc(sent, 1)
                    pool.wait_ge(sent, 1)
                    edge = r.sem("edge")
                    pool.dma_start(SRT[0:1, :], minus[0:1, :]).then_inc(edge, 16)
                    pool.dma_start(SRT[E + 1:E + 2, :], minus[0:1, :]).then_inc(edge, 16)
                    pool.wait_ge(placed, 1)
                    for c in range(NC):
                        if c >= 4:
                            pool.wait_ge(ring[c % 4], 16 * (c // 4))
                        pool.indirect_dma_start(
                            out=SRT[:, :], out_offset=bass.IndirectOffsetOnAxis(ap=where[:, c:c + 1], axis=0),
                            in_=rec[:, c, :], in_offset=None).then_inc(ring[c % 4], 16)
                    for i in range(4):
                        pool.wait_ge(ring[i], 16 * (NC // 4))
                    pool.wait_ge(edge, 32)

    with Phase(nc, name + "c") as ph:
        srt = ph.sb("srt", [HALF, 3, 2, EC, 2], I32)
        srf = ph.sb("srf", [HALF, 4, 2, EC])
        pack = ph.sb("pack", [HALF, 2, EC], I32)
        nxt = ph.sb("nxt", [EC, NC])
        prv = ph.sb("prv", [EC, NC])
        flag = ph.sb("flag", [EC, NC])
        tp = [ph.ps(f"tp{x}", [P, 512]) for x in range(4)]
        loaded, conv, turned, saved, rowed, chain = (
            ph.sem(x) for x in ("loaded", "conv", "turned", "saved", "rowed", "chain"))
        with nc.Block() as block:
            @block.sync
            def _(sp):
                for x, shift in enumerate((1, 2, 0)):
                    sp.dma_start(srt[:, x, :, :, :],
                                 SRT[shift:shift + E, :].rearrange("(a c p) w -> c a p w", a=2, p=EC))\
                      .then_inc(loaded, 16)
                sp.wait_ge(conv, 1)
                sp.dma_start(keys_dram.rearrange("(a c p) -> c a p", a=2, p=EC), pack[:, :, :]).then_inc(saved, 16)
                sp.wait_ge(saved, 16)
                sp.dma_start(keyrow[:, 1:1 + E],
                             keys_dram.rearrange("(a e) -> a e", a=1).broadcast_to([P, E])).then_inc(rowed, 16)
                sp.wait_ge(rowed, 16)

            @block.vector
            def _(dve):
                dve.wait_ge(loaded, 48)
                nc.vector.tensor_copy(pack[:, :, :], srt[:, 0, :, :, 0])
                nc.vector.tensor_copy(srf[:, 0, :, :], srt[:, 0, :, :, 0])
                nc.vector.tensor_copy(srf[:, 1, :, :], srt[:, 0, :, :, 1])
                nc.vector.tensor_copy(srf[:, 2, :, :], srt[:, 1, :, :, 0])
                nc.vector.tensor_copy(srf[:, 3, :, :], srt[:, 2, :, :, 0])
                nc.vector.memset(keyrow[:, 0:1], -1).then_inc(conv, 1)
                ch = Chain(dve, chain, 2)
                ch.start(0)
                dve.wait_ge(turned, 1)
                nc.vector.tensor_copy(t["key"][:, :], tp[0][0:EC, 0:NC])
                nc.vector.tensor_copy(t["keyint"][:, :], tp[0][0:EC, 0:NC])
                nc.vector.tensor_copy(t["other"][:, :], tp[1][0:EC, 0:NC])
                nc.vector.tensor_copy(prv[:, :], tp[3][0:EC, 0:NC])
                ch.link(nc.vector.tensor_copy(nxt[:, :], tp[2][0:EC, 0:NC]))
                ch.link(nc.vector.tensor_tensor(flag[:, :], t["key"][:, :], nxt[:, :], ALU.is_equal))
                nc.vector.scalar_tensor_tensor(t["row"][:, :], flag[:, :], SKIP, t["key"][:, :], ALU.mult,
                                               ALU.add)

            @block.tensor
            def _(pe):
                pe.wait_ge(conv, 1)
                for x in range(4):
                    for a in range(2):
                        last = nc.tensor.transpose(tp[x][0:EC, a * HALF:(a + 1) * HALF], srf[:, x, a, :],
                                                   k["ident"][0:HALF, 0:HALF])
                last.then_inc(turned, 1)


def target_scales(nc, k, deg):
    with Phase(nc, "scales") as ph:
        one = ph.sb("one", [P, NCOL])
        neg = ph.sb("neg", [P, NCOL])
        pair = ph.sb("pair", [P, NCOL, 2])
        got = ph.sb("got", [EC, NC, 2])
        made, ready, saved, gathered, chain = (ph.sem(x) for x in ("made", "ready", "saved", "gathered", "chain"))
        ring = [ph.sem(f"ring{i}") for i in range(4)]
        with nc.Block() as block:
            @block.vector
            def _(dve):
                ch = Chain(dve, chain, 3)
                ch.start(0)
                nc.vector.memset(neg[:, :], -0.5)
                ch.link(nc.vector.tensor_scalar(one[:, :], deg[:, :], 1.0, None, ALU.max))
                ch.link(nc.vector.reciprocal(pair[:, :, 0], one[:, :]))
                ch.link(nc.vector.tensor_scalar(one[:, :], deg[:, :], 1.0, None, ALU.add))
                nc.vector.memset(got[:, :, :], 0.0).then_inc(made, 1)
                ch.end()
                dve.wait_ge(ready, 1)
                nc.vector.tensor_copy(pair[:, :, 1], k["dinv"][:, :])
                nc.vector.tensor_tensor(k["dinv2"][:, :], k["dinv"][:, :], k["dinv"][:, :],
                                        ALU.mult).then_inc(ready, 1)
                dve.wait_ge(gathered, 1)
                nc.vector.tensor_copy(k["edge_invdeg"][:, :], got[:, :, 0])
                nc.vector.tensor_copy(k["edge_dinv"][:, :], got[:, :, 1])

            @block.sync
            def _(sp):
                sp.wait_ge(ready, 2)
                sp.dma_start(k["SCALE"].rearrange("(b p k) r -> p b (k r)", p=P, k=SUB),
                             pair[:, :, :].rearrange("p (b k) r -> p b (k r)", k=SUB)).then_inc(saved, 16)
                sp.wait_ge(saved, 16)

            @block.gpsimd
            def _(pool):
                pool.wait_ge(made, 1)
                nc.gpsimd.tensor_tensor(k["dinv"][:, :], one[:, :], neg[:, :], ALU.pow).then_inc(ready, 1)
                pool.wait_ge(saved, 16)
                for c in range(NC):
                    if c >= 4:
                        pool.wait_ge(ring[c % 4], 16 * (c // 4))
                    pool.indirect_dma_start(
                        out=got[:, c, :], out_offset=None, in_=k["SCALE"][:, :],
                        in_offset=bass.IndirectOffsetOnAxis(ap=k["by_dst"]["keyint"][:, c:c + 1], axis=0))\
                        .then_inc(ring[c % 4], 16)
                for i in range(4):
                    pool.wait_ge(ring[i], 16 * (NC // 4))
                nc.gpsimd.memset(k["spare"][:, :], 0.0).then_inc(gathered, 1)


RG = 8
RO = 4
LAG = 3


def edge_pass(nc, k, name, t, keyrow, kind, table, out_table, scale=None):
    W = D + H if kind == "attention" else D
    OW = 2 * D if kind == "sum_max" else D
    with Phase(nc, name) as ph:
        GW = 2 * D if kind == "attention" else D
        G = [ph.sb(f"G{u}", [EC, GW]) for u in range(RG)]
        same = ph.sb("same", [EC, 2, EC])
        carry = ph.sb("carry", [EC, 2, EC])
        tot = ph.sb("tot", [EC, 2, W])
        rows = [ph.sb(f"rows{u}", [EC, OW]) for u in range(RO)]
        psS = [ph.ps(f"psS{u}", [P, 512]) for u in range(2)]
        gat = [ph.sem(f"gat{u}") for u in range(RG)]
        sca = [ph.sem(f"sca{u}") for u in range(RO)]
        eq, summed, kept, out_ready = (ph.sem(x) for x in ("eq", "summed", "kept", "out_ready"))
        if kind == "attention":
            Q = [ph.sb(f"Q{u}", [EC, D]) for u in range(RG)]
            qgat = [ph.sem(f"qgat{u}") for u in range(RG)]
            prod = ph.sb("prod", [EC, 2, D])
            sc = ph.sb("sc", [EC, 2, H])
            msg = ph.sb("msg", [EC, 2, W])
            z = ph.sb("z", [EC, 2, H])
            clipped, scored, message = (ph.sem(x) for x in ("clipped", "scored", "message"))
        if kind == "sum_max":
            GT = ph.sb("GT", [P, 2, EC])
            MT = ph.sb("MT", [P, 2, EC])
            pen = ph.sb("pen", [P, 2, EC])
            head = ph.sb("head", [P, EC])
            psT = [ph.ps(f"psT{u}", [P, 512]) for u in range(2)]
            psM = [ph.ps(f"psM{u}", [P, 512]) for u in range(2)]
            turned, gtd, scanned, back = (ph.sem(x) for x in ("turned", "gtd", "scanned", "back"))
        chain, zed, penned = ph.sem("chain"), ph.sem("zed"), ph.sem("penned")

        with nc.Block() as block:
            @block.gpsimd
            def _(pool):
                for c in range(NC + LAG):
                    if c < NC:
                        if c >= RG:
                            pool.wait_ge(summed, c - RG + 1)
                        pool.indirect_dma_start(
                            out=G[c % RG][:, :], out_offset=None, in_=table,
                            in_offset=bass.IndirectOffsetOnAxis(ap=t["other"][:, c:c + 1], axis=0))\
                            .then_inc(gat[c % RG], 16)
                        if kind == "attention":
                            pool.indirect_dma_start(
                                out=Q[c % RG][:, :], out_offset=None, in_=k["QT"],
                                in_offset=bass.IndirectOffsetOnAxis(ap=t["keyint"][:, c:c + 1], axis=0))\
                                .then_inc(qgat[c % RG], 16)
                    if c >= LAG:
                        o = c - LAG
                        pool.wait_ge(out_ready, o + 1)
                        pool.indirect_dma_start(
                            out=out_table, out_offset=bass.IndirectOffsetOnAxis(ap=t["row"][:, o:o + 1], axis=0),
                            in_=rows[o % RO][:, :], in_offset=None, bounds_check=NPAD - 1, oob_is_err=False)\
                            .then_inc(sca[o % RO], 16)
                for u in range(RO):
                    pool.wait_ge(sca[u], 16 * (NC // RO))

            @block.vector
            def _(dve):
                ch = Chain(dve, chain, 2 if kind == "attention" else 1)

                def equal(c, u, q):
                    wait(dve, summed, c - 1)
                    here = keyrow[0:EC, bass.ds(c * EC + 1, EC)]
                    ins = nc.vector.tensor_scalar(same[:, u % 2, :], here, t["key"][:, bass.ds(c, 1)], None,
                                                  ALU.is_equal)
                    if not (isinstance(c, int) and c == 0):
                        ins = nc.vector.tensor_scalar(carry[:, u % 2, :], here, t["key"][:, bass.ds(c - 1, 1)],
                                                      k["lastrow"][0:EC, :], ALU.is_equal, ALU.mult)
                    ins.then_inc(eq, 1)

                def weigh(c, u, q):
                    dve.wait_ge(gat[u], 16 * (q + 1))
                    dve.wait_ge(qgat[u], 16 * (q + 1))
                    s = u % 2
                    ch.start(c)
                    ch.link(nc.vector.tensor_tensor(prod[:, s, :], G[u][:, 0:D], Q[u][:, :], ALU.mult))
                    ch.link(nc.vector.tensor_reduce(sc[:, s, :], prod[:, s, :].rearrange("e (h d) -> e h d", h=H),
                                                    AX.X, ALU.add))
                    ch.end()
                    lim = 5.0 * DH ** 0.5
                    nc.vector.tensor_scalar(sc[:, s, :], sc[:, s, :], lim, -lim, ALU.min,
                                            ALU.max).then_inc(clipped, 1)

                def messages(c, u, q):
                    s = u % 2
                    dve.wait_ge(scored, c + 1)
                    nc.vector.tensor_tensor(
                        msg[:, s, 0:D].rearrange("e (h d) -> e h d", h=H),
                        G[u][:, D:2 * D].rearrange("e (h d) -> e h d", h=H),
                        msg[:, s, D:W].unsqueeze(2).broadcast_to([EC, H, DH]), ALU.mult).then_inc(message, 1)

                def scan(c, u, q):
                    s = u % 2
                    wait(dve, back, c - 1)
                    ch.start(c)
                    ch.link(nc.vector.tensor_tensor(head[:, :], keyrow[:, bass.ds(c * EC + 1, EC)],
                                                    keyrow[:, bass.ds(c * EC, EC)], ALU.not_equal))
                    ch.end()
                    nc.vector.tensor_scalar(pen[:, s, :], head[:, :], NEG, None, ALU.mult).then_inc(penned, 1)
                    dve.wait_ge(penned, c + 1)
                    dve.wait_ge(gtd, c + 1)
                    wait(dve, scanned, c)
                    init = 0.0 if isinstance(c, int) and c == 0 else MT[:, 1 - s, EC - 1:EC]
                    nc.vector.tensor_tensor_scan(MT[:, s, :], pen[:, s, :], GT[:, s, :], init, ALU.add,
                                                 ALU.max).then_inc(scanned, 1)

                def finish(c, u, q):
                    s = u % 2
                    o = u % RO
                    dve.wait_ge(kept, c + 1)
                    back_q = q * (RG // RO) + u // RO
                    wait(dve, sca[o], 16 * back_q)
                    if kind == "sum":
                        nc.vector.tensor_scalar(rows[o][:, :], tot[:, s, 0:D], scale[:, bass.ds(c, 1)],
                                                None, ALU.mult).then_inc(out_ready, 1)
                    elif kind == "sum_max":
                        dve.wait_ge(back, c + 1)
                        nc.vector.tensor_copy(rows[o][:, 0:D], tot[:, s, 0:D])
                        nc.vector.tensor_copy(rows[o][:, D:2 * D], psM[s][0:EC, 0:D]).then_inc(out_ready, 1)
                    else:
                        nc.vector.tensor_scalar(z[:, s, :], tot[:, s, D:W], 1e-6, None,
                                                ALU.add).then_inc(zed, 1)
                        dve.wait_ge(zed, 2 * c + 1)
                        nc.vector.reciprocal(z[:, s, :], z[:, s, :]).then_inc(zed, 1)
                        dve.wait_ge(zed, 2 * c + 2)
                        nc.vector.tensor_tensor(
                            rows[o][:, :].rearrange("e (h d) -> e h d", h=H),
                            tot[:, s, 0:D].rearrange("e (h d) -> e h d", h=H),
                            z[:, s, :].unsqueeze(2).broadcast_to([EC, H, DH]), ALU.mult).then_inc(out_ready, 1)

                if kind == "sum":
                    steps(dve, [(0, equal), (1, finish)], NC, RG, RG, RG)
                elif kind == "sum_max":
                    steps(dve, [(0, equal), (0, scan), (1, finish)], NC, RG, RG, RG)
                else:
                    steps(dve, [(0, equal), (0, weigh), (1, messages), (2, finish)], NC, RG, RG, RG)

            @block.scalar
            def _(act):
                def turn(c, u, q):
                    act.wait_ge(turned, c + 1)
                    wait(act, scanned, c - 1)
                    nc.scalar.activation(GT[:, u % 2, :], psT[u % 2][:, 0:EC], ACT.Copy).then_inc(gtd, 1)

                def score(c, u, q):
                    act.wait_ge(clipped, c + 1)
                    wait(act, summed, c - 1)
                    nc.scalar.activation(msg[:, u % 2, D:W], sc[:, u % 2, :], ACT.Exp,
                                         scale=DH ** -0.5).then_inc(scored, 1)

                def keep(c, u, q):
                    act.wait_ge(summed, c + 1)
                    wait(act, out_ready, c - 1)
                    nc.scalar.activation(tot[:, u % 2, :], psS[u % 2][0:EC, 0:W], ACT.Copy).then_inc(kept, 1)
                stages = {"sum": [(1, keep)], "sum_max": [(0, turn), (1, keep)],
                          "attention": [(0, score), (2, keep)]}[kind]
                steps(act, stages, NC, RG, RG, RG)

            @block.tensor
            def _(pe):
                def turn(c, u, q):
                    pe.wait_ge(gat[u], 16 * (q + 1))
                    wait(pe, gtd, c - 1)
                    nc.tensor.transpose(psT[u % 2][:, 0:EC], G[u][:, :],
                                        k["ident"][0:EC, 0:EC]).then_inc(turned, 1)

                def turn_back(c, u, q):
                    pe.wait_ge(scanned, c + 1)
                    wait(pe, out_ready, c - 1)
                    nc.tensor.transpose(psM[u % 2][0:EC, 0:D], MT[:, u % 2, :],
                                        k["ident"][:, :]).then_inc(back, 1)

                def total(c, u, q):
                    s = u % 2
                    first = isinstance(c, int) and c == 0
                    pe.wait_ge(eq, c + 1)
                    if kind == "attention":
                        pe.wait_ge(message, c + 1)
                        values = msg[:, s, :]
                    else:
                        pe.wait_ge(gat[u], 16 * (q + 1))
                        values = G[u][:, :]
                    wait(pe, kept, c - 1)
                    ins = nc.tensor.matmul(psS[s][0:EC, 0:W], same[:, s, :], values, start=True, stop=first)
                    if not first:
                        pe.wait_ge(kept, c)
                        ins = nc.tensor.matmul(psS[s][0:EC, 0:W], carry[:, s, :], tot[:, 1 - s, :],
                                               start=False, stop=True)
                    ins.then_inc(summed, 1)
                if kind == "sum_max":
                    steps(pe, [(0, turn), (0, total), (1, turn_back)], NC, RG, RG, RG)
                elif kind == "attention":
                    steps(pe, [(1, total)], NC, RG, RG, RG)
                else:
                    steps(pe, [(0, total)], NC, RG, RG, RG)


def source_scales(nc, k, deg):
    with Phase(nc, "outscale") as ph:
        m, done = ph.sb("m", [P, NCOL]), ph.sem("done")
        with nc.Block() as block:
            @block.vector
            def _(dve):
                nc.vector.tensor_scalar(m[:, :], deg[:, :], 1.0, None, ALU.max).then_inc(done, 1)
                dve.wait_ge(done, 1)
                nc.vector.reciprocal(k["invcnt"][:, :], m[:, :])


def tile(ph, name, ring, width=D):
    return ph.sb(name, [P, ring, SUB, width])


def per_node(table, i):
    return table[:, bass.ds(i * SUB, SUB)].unsqueeze(2).broadcast_to([P, SUB, D])


def spread(row):
    return row[:, :].unsqueeze(1).broadcast_to([P, SUB, D])


def load_block(sp, dst, src, i, sem, real=False):
    if real and isinstance(i, int) and i == NB - 1:
        sp.dma_start(dst[0:TAILP, :, :], src[N - TAILP * SUB:N, :].rearrange("(p k) d -> p k d", k=SUB))\
          .then_inc(sem, 16)
    else:
        sp.dma_start(dst, block_of(src, i)).then_inc(sem, 16)


def store_block(sp, dst, src, i, sem, real=False):
    if real and isinstance(i, int) and i == NB - 1:
        sp.dma_start(dst[N - TAILP * SUB:N, :].rearrange("(p k) d -> p k d", k=SUB), src[0:TAILP, :, :])\
          .then_inc(sem, 16)
    else:
        sp.dma_start(block_of(dst, i), src).then_inc(sem, 16)


def block_of(ap, i):
    return ap[bass.ds(i * BLK, BLK), :].rearrange("(p k) d -> p k d", k=SUB)


RL = 4
HEAD, TAIL = 8, NB % RL
RY = 8


class Norm:

    def __init__(self, nc, ph, k, name):
        self.nc, self.k = nc, k
        self.st = ph.sb(name + "st", [P, 2, SUB, 6])
        self.mv = ph.sb(name + "mv", [P, 2, SUB, 2])
        self.ve = ph.sb(name + "ve", [P, 2, SUB])
        self.rs = ph.sb(name + "rs", [P, 2, SUB])
        self.carrier = ph.sb(name + "carrier", [P, 1])
        self.gathered = ph.sem(name + "gathered")
        self.measured = ph.sem(name + "measured")
        self.shifted = ph.sem(name + "shifted")
        self.rooted = ph.sem(name + "rooted")
        self.normed = ph.sem(name + "normed")

    def stats(self, dve, x, i, u):
        nc, s = self.nc, u % 2
        for m in range(SUB):
            last = nc.vector.bn_stats(self.st[:, s, m, :], x[:, m, :])
        last.then_inc(self.gathered, 1)
        dve.wait_ge(self.gathered, i + 1)
        wait(dve, self.normed, i - 1)
        nc.vector.tensor_copy(self.carrier[:, :], self.k["half"][:, 0:1])
        for m in range(SUB):
            last = nc.vector.bn_aggr(self.mv[:, s, m, :], self.st[:, s, m, :])
        last.then_inc(self.measured, 1)

    def root(self, pool, i, u):
        nc, s = self.nc, u % 2
        pool.wait_ge(self.measured, i + 1)
        nc.gpsimd.tensor_tensor(self.ve[:, s, :], self.mv[:, s, :, 1], self.k["eps"][:, :], ALU.add)\
            .then_inc(self.shifted, 1)
        pool.wait_ge(self.shifted, i + 1)
        wait(pool, self.normed, i - 1)
        nc.gpsimd.tensor_tensor(self.rs[:, s, :], self.ve[:, s, :], self.k["half"][:, :],
                                ALU.pow).then_inc(self.rooted, 1)

    def apply(self, dve, out, x, i, u):
        nc, s = self.nc, u % 2
        dve.wait_ge(self.rooted, i + 1)
        for m in range(SUB):
            last = nc.vector.tensor_scalar(out[:, m, :], x[:, m, :], self.mv[:, s, m, 0:1],
                                           self.rs[:, s, m:m + 1], ALU.subtract, ALU.mult)
        last.then_inc(self.normed, 1)


def first_norm(nc, k, x_in, h_out):
    with Phase(nc, "ln0") as ph:
        X, Hh = tile(ph, "X", RL), tile(ph, "H", RL)
        ld = [ph.sem(f"ld{u}") for u in range(RL)]
        st = [ph.sem(f"st{u}") for u in range(RL)]
        relud, zeroed = ph.sem("relud"), ph.sem("zeroed")
        ln = Norm(nc, ph, k, "n")
        with nc.Block() as block:
            @block.sync
            def _(sp):
                def load(i, u, q):
                    alone(sp, ln.normed, i - RL + 1)
                    load_block(sp, X[:, u, :, :], x_in, i, ld[u], real=True)
                steps(sp, [(0, load)], NB, RL, HEAD, TAIL)

            @block.vector
            def _(dve):
                def stats(i, u, q):
                    dve.wait_ge(ld[u], 16 * (q + 1))
                    ln.stats(dve, X[:, u, :, :], i, u)

                def apply(i, u, q):
                    wait(dve, st[u], 16 * q)
                    ln.apply(dve, Hh[:, u, :, :], X[:, u, :, :], i, u)
                steps(dve, [(0, stats), (1, apply)], NB, RL, HEAD, TAIL)

            @block.gpsimd
            def _(pool):
                steps(pool, [(0, lambda i, u, q: ln.root(pool, i, u))], NB, RL, HEAD, TAIL)

            @block.scalar
            def _(act):
                def relu(i, u, q):
                    act.wait_ge(ln.normed, i + 1)
                    nc.scalar.activation(Hh[:, u, :, :], Hh[:, u, :, :], ACT.Relu).then_inc(relud, 1)

                def store(i, u, q):
                    act.wait_ge(relud, i + 1)
                    store_block(act, h_out, Hh[:, u, :, :], i, st[u])
                steps(act, [(0, relu), (1, store)], NB, RL, HEAD, TAIL)
                for u in range(RL):
                    act.wait_ge(st[u], 16 * len(range(u, NB, RL)))


def conv_layer(nc, k, name, kind, agg, h_in, w_agg, w_self, bias, self_bias=None, h_out=None, g_out=None,
               x_in=None, x_out=None, x_real=False):
    gcn = kind == "gcn"
    proj = gcn and w_self is not None
    turn_h = w_self is not None
    ends = x_in is not None
    with Phase(nc, name) as ph:
        A, Hi = tile(ph, "A", RL), tile(ph, "Hi", RL)
        ROUT, RGO = (2 if ends else RL), 2
        O = tile(ph, "O", ROUT)
        if ends:
            X, X1, Hn = tile(ph, "X", RL), tile(ph, "X1", RL), tile(ph, "Hn", RL)
            ln = Norm(nc, ph, k, "n")
        if g_out is not None:
            Go = tile(ph, "Go", RGO)
        aT, hT = ph.sb("aT", [P, 2, BLK]), ph.sb("hT", [P, 2, BLK]) if turn_h else None
        pre = ph.sb("pre", [P, 2, SUB, D])
        pre2 = ph.sb("pre2", [P, 2, SUB, D]) if proj else None
        psA = [ph.ps(f"psA{u}", [P, BLK]) for u in range(2)]
        psH = [ph.ps(f"psH{u}", [P, BLK]) for u in range(2)] if turn_h else None
        psO = [ph.ps(f"psO{u}", [P, BLK]) for u in range(2)]
        psR = [ph.ps(f"psR{u}", [P, BLK]) for u in range(2)] if proj else None
        la, lh, lx, so, sx, sg = ([ph.sem(f"{x}{u}") for u in range(RL)] for x in ("la", "lh", "lx", "so", "sx", "sg"))
        mixed, turned, evA, evH, mult, biased, acted, joined, scaled, relud = (
            ph.sem(x) for x in ("mixed", "turned", "evA", "evH", "mult", "biased", "acted", "joined",
                                "scaled", "relud"))
        out_done = joined if (proj or ends) else acted
        with nc.Block() as block:
            @block.sync
            def _(sp):
                def load(i, u, q):
                    alone(sp, turned, i - RL + 1)
                    load_block(sp, A[:, u, :, :], agg, i, la[u])
                    load_block(sp, Hi[:, u, :, :], h_in, i, lh[u])

                def load_x(i, u, q):
                    alone(sp, joined, i - RL + 1)
                    load_block(sp, X[:, u, :, :], x_in, i, lx[u], real=x_real)

                steps(sp, [(0, load), (0, load_x)] if ends else [(0, load)], NB, RL, HEAD, TAIL)

            @block.tensor
            def _(pe):
                def turn(i, u, q):
                    s = u % 2
                    pe.wait_ge(lh[u], 16 * (q + 1))
                    if gcn:
                        pe.wait_ge(mixed, i + 1)
                    else:
                        pe.wait_ge(la[u], 16 * (q + 1))
                    wait(pe, evA, i - 1)
                    if turn_h:
                        wait(pe, evH, i - 1)
                    for m in range(SUB):
                        last = nc.tensor.transpose(psA[s][:, m * P:(m + 1) * P], A[:, u, m, :], k["ident"][:, :])
                    if turn_h:
                        for m in range(SUB):
                            last = nc.tensor.transpose(psH[s][:, m * P:(m + 1) * P], Hi[:, u, m, :],
                                                       k["ident"][:, :])
                    last.then_inc(turned, 1)

                def multiply(i, u, q):
                    s = u % 2
                    pe.wait_ge(evA, i + 1)
                    if turn_h:
                        pe.wait_ge(evH, i + 1)
                    wait(pe, biased, i - 1)
                    for m in range(SUB):
                        cols = slice(m * P, (m + 1) * P)
                        last = nc.tensor.matmul(psO[s][:, cols], aT[:, s, cols], w_agg, start=True,
                                                stop=not turn_h or proj)
                        if turn_h:
                            last = nc.tensor.matmul(psR[s][:, cols] if proj else psO[s][:, cols],
                                                    hT[:, s, cols], w_self, start=proj, stop=True)
                    last.then_inc(mult, 1)
                steps(pe, [(0, turn), (1, multiply)], NB, RL, HEAD, TAIL)

            @block.vector
            def _(dve):
                def mix(i, u, q):
                    dve.wait_ge(la[u], 16 * (q + 1))
                    dve.wait_ge(lh[u], 16 * (q + 1))
                    for m in range(SUB):
                        last = nc.vector.scalar_tensor_tensor(
                            A[:, u, m, :], Hi[:, u, m, :], k["dinv2"][:, bass.ds(i * SUB + m, 1)],
                            A[:, u, m, :], ALU.mult, ALU.add)
                    last.then_inc(mixed, 1)

                def evacuate(i, u, q):
                    dve.wait_ge(turned, i + 1)
                    wait(dve, mult, i - 1)
                    nc.vector.tensor_copy(aT[:, u % 2, :], psA[u % 2][:, :]).then_inc(evA, 1)

                def add_bias(i, u, q):
                    s = u % 2
                    dve.wait_ge(mult, i + 1)
                    wait(dve, acted, i - 1)
                    if proj:
                        wait(dve, joined, i - 1)
                        nc.vector.tensor_tensor(pre2[:, s, :, :], psR[s][:, :].rearrange("p (k d) -> p k d", k=SUB),
                                                spread(self_bias), ALU.add)
                    nc.vector.tensor_tensor(pre[:, s, :, :], psO[s][:, :].rearrange("p (k d) -> p k d", k=SUB),
                                            spread(bias), ALU.add).then_inc(biased, 1)

                def leak(i, u, q):
                    dve.wait_ge(biased, i + 1)
                    if ends:
                        wait(dve, joined, i - ROUT + 1)
                    else:
                        wait(dve, so[u], 16 * q)
                    nc.vector.scalar_tensor_tensor(O[:, u % ROUT, :, :], pre[:, u % 2, :, :], LEAK, pre[:, u % 2, :, :],
                                                   ALU.mult, ALU.max).then_inc(acted, 1)

                def stats(i, u, q):
                    dve.wait_ge(joined, i + 1)
                    ln.stats(dve, X1[:, u, :, :], i, u)

                def apply(i, u, q):
                    wait(dve, so[u], 16 * q)
                    if g_out is not None:
                        wait(dve, scaled, i - RL + 1)
                    ln.apply(dve, Hn[:, u, :, :], X1[:, u, :, :], i, u)
                stages = [(0, evacuate), (1, add_bias)]
                stages = [(0, mix)] + stages if gcn else stages + [(2, leak)]
                if ends:
                    stages += [(3, stats), (4, apply)]
                steps(dve, stages, NB, RL, HEAD, TAIL)

            @block.scalar
            def _(act):
                def evacuate(i, u, q):
                    act.wait_ge(turned, i + 1)
                    wait(act, mult, i - 1)
                    nc.scalar.activation(hT[:, u % 2, :], psH[u % 2][:, :], ACT.Copy).then_inc(evH, 1)

                def activate(i, u, q):
                    act.wait_ge(biased, i + 1)
                    if ends:
                        wait(act, joined, i - ROUT + 1)
                    else:
                        wait(act, so[u], 16 * q)
                        if g_out is not None:
                            wait(act, scaled, i - RL + 1)
                    nc.scalar.activation(O[:, u % ROUT, :, :], pre[:, u % 2, :, :], ACT.Relu).then_inc(acted, 1)

                def relu(i, u, q):
                    act.wait_ge(ln.normed, i + 1)
                    nc.scalar.activation(Hn[:, u, :, :], Hn[:, u, :, :], ACT.Relu).then_inc(relud, 1)
                stages = [(0, evacuate)] if turn_h else []
                if gcn:
                    stages += [(1, activate)]
                def store_x(i, u, q):
                    act.wait_ge(joined, i + 1)
                    store_block(act, x_out, X1[:, u, :, :], i, sx[u])

                def store_h(i, u, q):
                    act.wait_ge(relud if ends else out_done, i + 1)
                    store_block(act, h_out, (Hn if ends else O)[:, u, :, :], i, so[u])

                def store_g(i, u, q):
                    act.wait_ge(scaled, i + 1)
                    store_block(act, g_out, Go[:, u % RGO, :, :], i, sg[u % RGO])
                if ends:
                    stages += [(5, relu), (3, store_x), (6, store_h)]
                else:
                    stages += [(3, store_h)]
                if g_out is not None:
                    stages.append((7 if ends else 4, store_g))
                steps(act, stages, NB, RL, HEAD, TAIL)
                for u in range(RL):
                    count = 16 * len(range(u, NB, RL))
                    act.wait_ge(so[u], count)
                    if ends:
                        act.wait_ge(sx[u], count)
                if g_out is not None:
                    for u in range(RGO):
                        act.wait_ge(sg[u], 16 * (NB // RGO))

            @block.gpsimd
            def _(pool):
                def join(i, u, q):
                    pool.wait_ge(acted, i + 1)
                    if ends:
                        pool.wait_ge(lx[u], 16 * (q + 1))
                        wait(pool, sx[u], 16 * q)
                        wait(pool, ln.normed, i - RL + 1)
                        nc.gpsimd.tensor_tensor(X1[:, u, :, :], X[:, u, :, :], O[:, u % ROUT, :, :],
                                                ALU.add).then_inc(joined, 1)
                    else:
                        nc.gpsimd.tensor_tensor(O[:, u, :, :], O[:, u, :, :], pre2[:, u % 2, :, :],
                                                ALU.add).then_inc(joined, 1)

                def root(i, u, q):
                    ln.root(pool, i, u)

                def scale(i, u, q):
                    src = Hn if ends else O
                    pool.wait_ge(relud if ends else out_done, i + 1)
                    wait(pool, sg[u % RGO], 16 * (q * (RL // RGO) + u // RGO))
                    nc.gpsimd.tensor_tensor(Go[:, u % RGO, :, :], src[:, u, :, :], per_node(k["dinv"], i),
                                            ALU.mult).then_inc(scaled, 1)
                stages = []
                if proj or ends:
                    stages += [(2, join)]
                if ends:
                    stages += [(3, root)]
                if g_out is not None:
                    stages += [(6 if ends else 3, scale)]
                if stages:
                    steps(pool, stages, NB, RL, HEAD, TAIL)


def mlp_block(nc, k, h_in, agg2, x_in, x_out, h_out):
    with Phase(nc, "mlp") as ph:
        Hi, X, S2, M = tile(ph, "Hi", RL), tile(ph, "X", RL), tile(ph, "S2", 2, 2 * D), tile(ph, "M", 2)
        Y, Hn = tile(ph, "Y", 2), tile(ph, "Hn", 2)
        XT = ph.sb("XT", [P, 2, 4, BLK])
        HT = ph.sb("HT", [P, 2, HG, BLK])
        ln = Norm(nc, ph, k, "n")
        psT = [ph.ps(f"psT{u}", [P, BLK]) for u in range(2)]
        psH = [ph.ps(f"psH{u}", [P, BLK]) for u in range(2)]
        psO = [ph.ps(f"psO{u}", [P, BLK]) for u in range(2)]
        lh, lx, sx = ([ph.sem(f"{x}{u}") for u in range(RL)] for x in ("lh", "lx", "sx"))
        ls, so = ([ph.sem(f"{x}{u}") for u in range(2)] for x in ("ls", "so"))
        meaned, turned, evD, evA, hidden, relud1, mult, biased, joined, relud = (
            ph.sem(x) for x in ("meaned", "turned", "evD", "evA", "hidden", "relud1", "mult", "biased",
                                "joined", "relud"))
        plus = ph.sem("plus")
        with nc.Block() as block:
            @block.sync
            def _(sp):
                def load(i, u, q):
                    alone(sp, turned, 4 * (i - 1))
                    load_block(sp, S2[:, u % 2, :, :], agg2, i, ls[u % 2])
                    alone(sp, joined, i - RL + 1)
                    load_block(sp, Hi[:, u, :, :], h_in, i, lh[u])

                def load_x(i, u, q):
                    alone(sp, sx[u], 16 * q, 16)
                    load_block(sp, X[:, u, :, :], x_in, i, lx[u])

                steps(sp, [(0, load), (3, load_x)], NB, RL, HEAD, TAIL)

            @block.gpsimd
            def _(pool):
                def mean(i, u, q):
                    s = u % 2
                    pool.wait_ge(ls[s], 16 * (2 * q + u // 2 + 1))
                    wait(pool, turned, 4 * (i - 1))
                    nc.gpsimd.tensor_tensor(M[:, s, :, :], S2[:, s, :, 0:D], per_node(k["invcnt"], i),
                                            ALU.mult).then_inc(meaned, 1)

                def join(i, u, q):
                    pool.wait_ge(biased, i + 1)
                    pool.wait_ge(lx[u], 16 * (q + 1))
                    nc.gpsimd.tensor_tensor(Y[:, u % 2, :, :], Y[:, u % 2, :, :], Hi[:, u, :, :],
                                            ALU.add).then_inc(plus, 1)
                    pool.wait_ge(plus, i + 1)
                    nc.gpsimd.tensor_tensor(X[:, u, :, :], X[:, u, :, :], Y[:, u % 2, :, :],
                                            ALU.add).then_inc(joined, 1)

                def root(i, u, q):
                    ln.root(pool, i, u)
                steps(pool, [(0, mean), (3, join), (4, root)], NB, RL, HEAD, TAIL)

            @block.tensor
            def _(pe):
                def turn(i, u, q):
                    s = u % 2
                    for b in range(4):
                        if b == 0:
                            pe.wait_ge(lh[u], 16 * (q + 1))
                            src = Hi[:, u, :, :]
                        elif b == 1:
                            pe.wait_ge(ls[s], 16 * (2 * q + u // 2 + 1))
                            src = S2[:, s, :, 0:D]
                        elif b == 2:
                            src = S2[:, s, :, D:2 * D]
                        else:
                            pe.wait_ge(meaned, i + 1)
                            src = M[:, s, :, :]
                        wait(pe, evA if b % 2 else evD, 2 * i + b // 2)
                        for m in range(SUB):
                            last = nc.tensor.transpose(psT[b % 2][:, m * P:(m + 1) * P], src[:, m, :],
                                                       k["ident"][:, :])
                        last.then_inc(turned, 1)

                def hide(i, u, q):
                    for g in range(HG):
                        wait(pe, relud1, HG * i + g - 1)
                        for b in range(4):
                            if g == 0:
                                pe.wait_ge(evA if b % 2 else evD, 2 * i + b // 2 + 1)
                            last = nc.tensor.matmul(psH[g % 2][:, :], k["m_w1"][:, b, g * P:(g + 1) * P],
                                                    XT[:, u % 2, b, :], start=b == 0, stop=b == 3)
                        last.then_inc(hidden, 1)

                def out(i, u, q):
                    s = u % 2
                    pe.wait_ge(relud1, HG * (i + 1))
                    wait(pe, biased, i - 1)
                    for m in range(SUB):
                        for g in range(HG):
                            last = nc.tensor.matmul(psO[s][:, m * P:(m + 1) * P], HT[:, s, g, m * P:(m + 1) * P],
                                                    k["m_w2"][:, g, :], start=g == 0, stop=g == HG - 1)
                    last.then_inc(mult, 1)
                steps(pe, [(0, turn), (1, hide), (2, out)], NB, RL, HEAD, TAIL)

            @block.vector
            def _(dve):
                def evacuate(i, u, q):
                    for b in (0, 2):
                        dve.wait_ge(turned, 4 * i + b + 1)
                        wait(dve, hidden, HG * (i - 1))
                        nc.vector.tensor_copy(XT[:, u % 2, b, :], psT[0][:, :]).then_inc(evD, 1)

                def add_bias(i, u, q):
                    dve.wait_ge(mult, i + 1)
                    wait(dve, joined, i - 1)
                    nc.vector.tensor_tensor(Y[:, u % 2, :, :], psO[u % 2][:, :].rearrange("p (k d) -> p k d", k=SUB),
                                            spread(k["m_b2"]), ALU.add).then_inc(biased, 1)

                def stats(i, u, q):
                    dve.wait_ge(joined, i + 1)
                    ln.stats(dve, X[:, u, :, :], i, u)

                def apply(i, u, q):
                    wait(dve, so[u % 2], 16 * (2 * q + u // 2))
                    ln.apply(dve, Hn[:, u % 2, :, :], X[:, u, :, :], i, u)
                steps(dve, [(0, evacuate), (2, add_bias), (4, stats), (5, apply)], NB, RL, HEAD, TAIL)

            @block.scalar
            def _(act):
                def evacuate(i, u, q):
                    for b in (1, 3):
                        act.wait_ge(turned, 4 * i + b + 1)
                        wait(act, hidden, HG * (i - 1))
                        nc.scalar.activation(XT[:, u % 2, b, :], psT[1][:, :], ACT.Copy).then_inc(evA, 1)

                def activate(i, u, q):
                    wait(act, mult, i - 1)
                    for g in range(HG):
                        act.wait_ge(hidden, HG * i + g + 1)
                        nc.scalar.activation(HT[:, u % 2, g, :], psH[g % 2][:, :], ACT.Relu,
                                             bias=k["m_b1"][:, g:g + 1]).then_inc(relud1, 1)

                def relu(i, u, q):
                    act.wait_ge(ln.normed, i + 1)
                    nc.scalar.activation(Hn[:, u % 2, :, :], Hn[:, u % 2, :, :], ACT.Relu).then_inc(relud, 1)

                def store_x(i, u, q):
                    act.wait_ge(ln.normed, i + 1)
                    store_block(act, x_out, X[:, u, :, :], i, sx[u])

                def store_h(i, u, q):
                    act.wait_ge(relud, i + 1)
                    store_block(act, h_out, Hn[:, u % 2, :, :], i, so[u % 2])
                steps(act, [(0, evacuate), (1, activate), (6, relu), (6, store_x), (7, store_h)],
                      NB, RL, HEAD, TAIL)
                for u in range(RL):
                    act.wait_ge(sx[u], 16 * len(range(u, NB, RL)))
                for u in range(2):
                    act.wait_ge(so[u], 16 * (NB // 2))


def project_qkv(nc, k, h_in):
    W3 = 3 * D
    with Phase(nc, "qkv") as ph:
        Hi = tile(ph, "Hi", RL)
        hT = ph.sb("hT", [P, 2, BLK])
        out = tile(ph, "out", RL, W3)
        psH = [ph.ps(f"psH{u}", [P, BLK]) for u in range(2)]
        psO = [ph.ps(f"psO{u}", [P, BLK]) for u in range(SUB)]
        ld, sq, sk = ([ph.sem(f"{x}{u}") for u in range(RL)] for x in ("ld", "sq", "sk"))
        turned, evH, mult, outD, outA = (ph.sem(x) for x in ("turned", "evH", "mult", "outD", "outA"))
        with nc.Block() as block:
            @block.sync
            def _(sp):
                def load(i, u, q):
                    alone(sp, turned, i - RL + 1)
                    load_block(sp, Hi[:, u, :, :], h_in, i, ld[u])

                steps(sp, [(0, load)], NB, RL, HEAD, TAIL)

            @block.tensor
            def _(pe):
                def turn(i, u, q):
                    pe.wait_ge(ld[u], 16 * (q + 1))
                    wait(pe, evH, i - 1)
                    for m in range(SUB):
                        last = nc.tensor.transpose(psH[u % 2][:, m * P:(m + 1) * P], Hi[:, u, m, :],
                                                   k["ident"][:, :])
                    last.then_inc(turned, 1)

                def multiply(i, u, q):
                    pe.wait_ge(evH, i + 1)
                    for m in range(SUB):
                        wait(pe, outA if m % 2 else outD, i)
                        nc.tensor.matmul(psO[m][:, 0:W3], hT[:, u % 2, m * P:(m + 1) * P], k["w_qkv"][:, :],
                                         start=True, stop=True).then_inc(mult, 1)
                steps(pe, [(0, turn), (1, multiply)], NB, RL, HEAD, TAIL)

            def take(eng, copy, first, done):
                def f(i, u, q):
                    wait(eng, sq[u], 16 * q)
                    wait(eng, sk[u], 16 * q)
                    for m in range(first, SUB, 2):
                        eng.wait_ge(mult, SUB * i + m + 1)
                        last = copy(out[:, u, m, :], psO[m][:, 0:W3])
                    last.then_inc(done, 1)
                return f

            @block.vector
            def _(dve):
                steps(dve, [(1, take(dve, nc.vector.tensor_copy, 0, outD))], NB, RL, HEAD, TAIL)

            @block.scalar
            def _(act):
                def evacuate(i, u, q):
                    act.wait_ge(turned, i + 1)
                    wait(act, mult, SUB * (i - 1))
                    nc.scalar.activation(hT[:, u % 2, :], psH[u % 2][:, :], ACT.Copy).then_inc(evH, 1)

                def copy(o, x):
                    return nc.scalar.activation(o, x, ACT.Copy)

                def store(i, u, q):
                    act.wait_ge(outD, i + 1)
                    act.wait_ge(outA, i + 1)
                    store_block(act, k["QT"], out[:, u, :, 0:D], i, sq[u])
                    store_block(act, k["KV"], out[:, u, :, D:W3], i, sk[u])
                steps(act, [(0, evacuate), (1, take(act, copy, 1, outA)), (2, store)], NB, RL, HEAD, TAIL)
                for u in range(RL):
                    act.wait_ge(sq[u], 16 * len(range(u, NB, RL)))
                    act.wait_ge(sk[u], 16 * len(range(u, NB, RL)))


def last_block(nc, k, agg, h_in, x_in, out):
    with Phase(nc, "last") as ph:
        A, Hi = tile(ph, "A", 2), tile(ph, "Hi", RL)
        X = tile(ph, "X", RY)
        Y = tile(ph, "Y", RY)
        Z = tile(ph, "Z", RY)
        aT, yT = ph.sb("aT", [P, 2, BLK]), ph.sb("yT", [P, 2, BLK])
        F = ph.sb("F", [P, 2, FG, BLK])
        n1, n2 = Norm(nc, ph, k, "n1"), Norm(nc, ph, k, "n2")
        psA, psY = (ph.ps(x, [P, BLK]) for x in ("psA", "psY"))
        psO, psF = ([ph.ps(f"{x}{u}", [P, BLK]) for u in range(2)] for x in ("psO", "psF"))
        psH = [ph.ps(f"psH{g}", [P, BLK]) for g in range(FG)]
        la = [ph.sem(f"la{u}") for u in range(2)]
        lh = [ph.sem(f"lh{u}") for u in range(RL)]
        lx, so = ([ph.sem(f"{x}{u}") for u in range(RY)] for x in ("lx", "so"))
        (turned, evA, attn, prepared, gained, ready, yturned, evY, hidden, relud, ffn, biased2, prepared2,
         gained2, shifted2, done, biased) = (
            ph.sem(x) for x in ("turned", "evA", "attn", "prepared", "gained", "ready", "yturned", "evY",
                                "hidden", "relud", "ffn", "biased2", "prepared2", "gained2", "shifted2",
                                "done", "biased"))
        four = lambda ps: ps[:, :].rearrange("p (k d) -> p k d", k=SUB)
        with nc.Block() as block:
            @block.sync
            def _(sp):
                def load(i, u, q):
                    alone(sp, turned, i - 1)
                    load_block(sp, A[:, u % 2, :, :], agg, i, la[u % 2])
                    alone(sp, biased, i - RL + 1)
                    load_block(sp, Hi[:, u % RL, :, :], h_in, i, lh[u % RL])

                def load_x(i, u, q):
                    alone(sp, done, i - RY + 1)
                    load_block(sp, X[:, u, :, :], x_in, i, lx[u])

                steps(sp, [(0, load), (4, load_x)], NB, RY, 2 * RY, NB % RY)

            @block.tensor
            def _(pe):
                def turn(i, u, q):
                    pe.wait_ge(la[u % 2], 16 * (q * (RY // 2) + u // 2 + 1))
                    wait(pe, evA, i)
                    for m in range(SUB):
                        last = nc.tensor.transpose(psA[:, m * P:(m + 1) * P], A[:, u % 2, m, :], k["ident"][:, :])
                    last.then_inc(turned, 1)

                def attend(i, u, q):
                    pe.wait_ge(evA, i + 1)
                    wait(pe, biased, i - 1)
                    for m in range(SUB):
                        last = nc.tensor.matmul(psO[u % 2][:, m * P:(m + 1) * P], aT[:, u % 2, m * P:(m + 1) * P],
                                                k["w_o"][:, :], start=True, stop=True)
                    last.then_inc(attn, 1)

                def turn_y(i, u, q):
                    pe.wait_ge(ready, i + 1)
                    wait(pe, evY, i)
                    for m in range(SUB):
                        last = nc.tensor.transpose(psY[:, m * P:(m + 1) * P], Y[:, u, m, :], k["ident"][:, :])
                    last.then_inc(yturned, 1)

                def hide(i, u, q):
                    pe.wait_ge(evY, i + 1)
                    for g in range(FG):
                        wait(pe, relud, FG * (i - 1) + g + 1)
                        nc.tensor.matmul(psH[g][:, :], k["f_w1"][:, g * P:(g + 1) * P], yT[:, u % 2, :],
                                         start=True, stop=True).then_inc(hidden, 1)

                def back(i, u, q):
                    pe.wait_ge(relud, FG * (i + 1))
                    wait(pe, biased2, i - 1)
                    for m in range(SUB):
                        for g in range(FG):
                            last = nc.tensor.matmul(psF[u % 2][:, m * P:(m + 1) * P], F[:, u % 2, g, m * P:(m + 1) * P],
                                                    k["f_w2"][:, g, :], start=g == 0, stop=g == FG - 1)
                    last.then_inc(ffn, 1)
                steps(pe, [(0, turn), (1, attend), (4, turn_y), (5, hide), (6, back)], NB, RY, 2 * RY, NB % RY)

            @block.vector
            def _(dve):
                def add_bias(i, u, q):
                    dve.wait_ge(attn, i + 1)
                    dve.wait_ge(prepared, i + 1)
                    wait(dve, prepared2, i - RY + 1)
                    nc.vector.tensor_tensor(Y[:, u, :, :], four(psO[u % 2]), Hi[:, u % RL, :, :],
                                            ALU.add).then_inc(biased, 1)

                def first(i, u, q):
                    dve.wait_ge(biased, i + 1)
                    n1.stats(dve, Y[:, u, :, :], i, u)

                def apply(i, u, q):
                    n1.apply(dve, Y[:, u, :, :], Y[:, u, :, :], i, u)
                    dve.wait_ge(n1.normed, i + 1)
                    nc.vector.tensor_tensor(Y[:, u, :, :], Y[:, u, :, :], spread(k["g1"]), ALU.mult)\
                        .then_inc(gained, 1)

                def evacuate(i, u, q):
                    dve.wait_ge(yturned, i + 1)
                    wait(dve, hidden, FG * (i - 1))
                    nc.vector.tensor_copy(yT[:, u % 2, :], psY[:, :]).then_inc(evY, 1)

                def add_bias2(i, u, q):
                    dve.wait_ge(ffn, i + 1)
                    dve.wait_ge(prepared2, i + 1)
                    nc.vector.tensor_tensor(Z[:, u, :, :], four(psF[u % 2]), Z[:, u, :, :], ALU.add)\
                        .then_inc(biased2, 1)

                def second(i, u, q):
                    dve.wait_ge(biased2, i + 1)
                    n2.stats(dve, Z[:, u, :, :], i, u)

                def apply2(i, u, q):
                    n2.apply(dve, Z[:, u, :, :], Z[:, u, :, :], i, u)
                steps(dve, [(1, add_bias), (2, first), (3, apply), (4, evacuate), (6, add_bias2), (7, second),
                            (8, apply2)], NB, RY, 2 * RY, NB % RY)

            @block.gpsimd
            def _(pool):
                def prepare(i, u, q):
                    pool.wait_ge(lh[u % RL], 16 * (q * (RY // RL) + u // RL + 1))
                    nc.gpsimd.tensor_tensor(Hi[:, u % RL, :, :], Hi[:, u % RL, :, :], spread(k["b_o"]), ALU.add)\
                        .then_inc(prepared, 1)

                def root(i, u, q):
                    n1.root(pool, i, u)

                def shift(i, u, q):
                    pool.wait_ge(gained, i + 1)
                    nc.gpsimd.tensor_tensor(Y[:, u, :, :], Y[:, u, :, :], spread(k["b1"]), ALU.add)\
                        .then_inc(ready, 1)

                def prepare2(i, u, q):
                    pool.wait_ge(ready, i + 1)
                    wait(pool, so[u], 16 * q)
                    nc.gpsimd.tensor_tensor(Z[:, u, :, :], Y[:, u, :, :], spread(k["f_b2"]), ALU.add)\
                        .then_inc(prepared2, 1)

                def root2(i, u, q):
                    n2.root(pool, i, u)

                def end(i, u, q):
                    pool.wait_ge(n2.normed, i + 1)
                    z = Z[:, u, :, :]
                    nc.gpsimd.tensor_tensor(z, z, spread(k["g2"]), ALU.mult).then_inc(gained2, 1)
                    pool.wait_ge(gained2, i + 1)
                    pool.wait_ge(shifted2, i + 1)
                    nc.gpsimd.tensor_tensor(z, z, X[:, u, :, :], ALU.add).then_inc(done, 1)

                def prepare3(i, u, q):
                    pool.wait_ge(lx[u], 16 * (q + 1))
                    nc.gpsimd.tensor_tensor(X[:, u, :, :], X[:, u, :, :], spread(k["b2"]), ALU.add)\
                        .then_inc(shifted2, 1)
                steps(pool, [(0, prepare), (2, root), (3, shift), (4, prepare2), (7, root2), (6, prepare3), (8, end)],
                      NB, RY, 2 * RY, NB % RY)

            @block.scalar
            def _(act):
                def evacuate(i, u, q):
                    act.wait_ge(turned, i + 1)
                    wait(act, attn, i - 1)
                    nc.scalar.activation(aT[:, u % 2, :], psA[:, :], ACT.Copy).then_inc(evA, 1)

                def activate(i, u, q):
                    wait(act, ffn, i - 1)
                    for g in range(FG):
                        act.wait_ge(hidden, FG * i + g + 1)
                        nc.scalar.activation(F[:, u % 2, g, :], psH[g][:, :], ACT.Relu,
                                             bias=k["f_b1"][:, g:g + 1]).then_inc(relud, 1)

                def store(i, u, q):
                    act.wait_ge(done, i + 1)
                    store_block(act, out, Z[:, u, :, :], i, so[u], real=True)
                steps(act, [(0, evacuate), (5, activate), (9, store)], NB, RY, 2 * RY, NB % RY)
                for u in range(RY):
                    act.wait_ge(so[u], 16 * len(range(u, NB, RY)))


def load_weights(nc, k, a):
    with Phase(nc, "weights") as ph:
        raw = ph.sb("raw", [P, 6, D])
        cols = ph.sb("cols", [P, 3, HG])
        us = ph.sb("us", [P, 1])
        ps = [ph.ps(f"ps{x}", [P, BLK]) for x in range(2)]
        loaded, turned = ph.sem("loaded"), ph.sem("turned")
        row = lambda v: v.rearrange("(a n) -> a n", a=1).broadcast_to([P, D])
        loads = [(raw[:, 0, :], a["L0_gnn_Wl1"]), (raw[:, 1, :], a["L0_gnn_Wr1"])]
        for n in range(2):
            loads += [(raw[:, 2 + 2 * n, :], a["L0_gnn_Wlh"][n, :, :]), (raw[:, 3 + 2 * n, :], a["L0_gnn_Wrh"][n, :, :])]
        loads += [(k["s_b"][0][:, :], row(a["L0_gnn_bl1"])), (k["s_b"][1][:, :], row(a["L0_gnn_blh"][0, :])),
                  (k["s_b"][2][:, :], row(a["L0_gnn_blh"][1, :]))]
        for n, (w, b) in enumerate((("W0", "b0"), ("W1", "b1"), ("W2", "b2"), ("Wr", "br"))):
            loads += [(k["g_w"][:, n, :], a["L1_gnn_" + w]), (k["g_b"][n][:, :], row(a["L1_gnn_" + b]))]
        loads += [(k["m_w1"][:, :, :], a["L2_gnn_W1"][0:4 * D, :].rearrange("(b p) n -> p b n", p=P)),
                  (k["m_w2"][:, :, :], a["L2_gnn_W2"].rearrange("(g p) n -> p g n", p=P)),
                  (k["m_b2"][:, :], row(a["L2_gnn_b2"])),
                  (us[:, :], a["L2_gnn_u"][0:1, :].broadcast_to([P, 1]))]
        for n, w in enumerate(("Wq", "Wk", "Wv")):
            loads += [(k["w_qkv"][:, n * D:(n + 1) * D], a["L3_gnn_" + w])]
        loads += [(k["w_o"][:, :], a["L3_gnn_Wo"]), (k["b_o"][:, :], row(a["L3_gnn_bo"])),
                  (k["f_w1"][:, :], a["L3_gnn_W1"]),
                  (k["f_w2"][:, :, :], a["L3_gnn_W2"].rearrange("(g p) n -> p g n", p=P)),
                  (k["f_b2"][:, :], row(a["L3_gnn_b2"])),
                  (k["g1"][:, :], row(a["L3_gnn_ln1_g"])), (k["b1"][:, :], row(a["L3_gnn_ln1_b"])),
                  (k["g2"][:, :], row(a["L3_gnn_ln2_g"])), (k["b2"][:, :], row(a["L3_gnn_ln2_b"]))]
        thin = [(cols[:, 0, :], a["L2_gnn_b1"].rearrange("(g p) -> p g", p=P)),
                (cols[:, 1, :], a["L2_gnn_W1"][4 * D, :].rearrange("(g p) -> p g", p=P)),
                (k["f_b1"][:, :], a["L3_gnn_b1"].rearrange("(g p) -> p g", p=P))]
        total = 16 * (len(loads) + len(thin))
        with nc.Block() as block:
            @block.sync
            def _(sp):
                for dst, src in loads:
                    sp.dma_start(dst, src).then_inc(loaded, 16)
                with nc.allow_non_contiguous_dma(reason="a few hundred bias elements, once"):
                    for dst, src in thin:
                        sp.dma_start(dst, src).then_inc(loaded, 16)
                sp.wait_ge(loaded, total)

            @block.tensor
            def _(pe):
                pe.wait_ge(loaded, total)
                for n in range(6):
                    last = nc.tensor.transpose(ps[n // 4][:, n % 4 * P:(n % 4 + 1) * P], raw[:, n, :],
                                               k["ident"][:, :])
                last.then_inc(turned, 1)

            @block.vector
            def _(dve):
                dve.wait_ge(loaded, total)
                nc.vector.scalar_tensor_tensor(k["m_b1"][:, :], cols[:, 1, :], us[:, :], cols[:, 0, :],
                                               ALU.mult, ALU.add)
                dve.wait_ge(turned, 1)
                for n in range(6):
                    nc.vector.tensor_copy(k["s_w"][:, n, :], ps[n // 4][:, n % 4 * P:(n % 4 + 1) * P])


def gnn_kernel(nc, a, out):
    with ExitStack() as ctx:
        def sb(name, shape, dt=F32):
            return ctx.enter_context(nc.sbuf_tensor(name, shape, dt))

        def dram(name, shape, dt=F32):
            return nc.dram_tensor(name, shape, dt, kind="Internal").ap()

        k = {
            "ident": sb("ident", [P, P]), "identb": sb("identb", [P, P], BF16),
            "before": sb("before", [P, P]), "upper": sb("upper", [P, P]), "lastrow": sb("lastrow", [P, 1]),
            "half": sb("half", [P, SUB]), "eps": sb("eps", [P, SUB]), "spare": sb("spare", [P, 1]),
            "dinv": sb("dinv", [P, NCOL]), "dinv2": sb("dinv2", [P, NCOL]), "invcnt": sb("invcnt", [P, NCOL]),
            "edge_invdeg": sb("edge_invdeg", [EC, NC]), "edge_dinv": sb("edge_dinv", [EC, NC]),
            "s_w": sb("s_w", [P, 6, D]), "s_b": [sb(f"s_b{n}", [P, D]) for n in range(3)],
            "g_w": sb("g_w", [P, 4, D]), "g_b": [sb(f"g_b{n}", [P, D]) for n in range(4)],
            "m_w1": sb("m_w1", [P, 4, HID]), "m_w2": sb("m_w2", [P, HG, D]), "m_b1": sb("m_b1", [P, HG]),
            "m_b2": sb("m_b2", [P, D]),
            "w_qkv": sb("w_qkv", [P, 3 * D]), "w_o": sb("w_o", [P, D]), "b_o": sb("b_o", [P, D]),
            "f_w1": sb("f_w1", [P, DFF]), "f_w2": sb("f_w2", [P, FG, D]), "f_b1": sb("f_b1", [P, FG]),
            "f_b2": sb("f_b2", [P, D]), "g1": sb("g1", [P, D]), "b1": sb("b1", [P, D]),
            "g2": sb("g2", [P, D]), "b2": sb("b2", [P, D]),
            "AGG": dram("AGG", (NPAD, D)), "AGG2": dram("AGG2", (NPAD, 2 * D)),
            "QT": dram("QT", (NPAD, D)), "KV": dram("KV", (NPAD, 2 * D)), "SCALE": dram("SCALE", (NPAD, 2)),
        }
        HA, HB, GA = dram("HA", (NPAD, D)), dram("HB", (NPAD, D)), dram("GA", (NPAD, D))
        X1, X2 = dram("X1", (NPAD, D)), dram("X2", (NPAD, D))
        lists = {}
        for name in ("by_dst", "by_src"):
            lists[name] = {"key": sb(name + "key", [EC, NC]), "keyint": sb(name + "keyint", [EC, NC], I32),
                           "other": sb(name + "other", [EC, NC], I32), "row": sb(name + "row", [EC, NC], I32)}
        k.update(lists)
        AGG, AGG2 = k["AGG"], k["AGG2"]

        def sort(name, key, other, deg, keyrow):
            sort_edges(nc, k, "sort_" + name, key, other, dram("SRT_" + name, (E + 2, 2), I32), deg,
                       dram("KEYS_" + name, (E,), I32), keyrow, lists[name])

        with ExitStack() as early:
            for name, shape in (("count", [P, NCOL]), ("one", [P, NCOL]), ("start", [P, NCOL])):
                k[name] = early.enter_context(nc.sbuf_tensor(name, shape, F32))
            deg = early.enter_context(nc.sbuf_tensor("deg", [P, NCOL], F32))
            keyrow = early.enter_context(nc.sbuf_tensor("keyrow_src", [P, 1 + E], I32))
            constants(nc, k)
            load_weights(nc, k, a)
            sort("by_src", a["src"], None, deg, keyrow)
            source_scales(nc, k, deg)
            edge_pass(nc, k, "agg_edges", lists["by_src"], keyrow, "sum_max", a["edge_attr_128"], AGG2)
        target_keys = ExitStack()
        keyrow = target_keys.enter_context(nc.sbuf_tensor("keyrow", [P, 1 + E], I32))
        with ExitStack() as early:
            for name, shape in (("count", [P, NCOL]), ("one", [P, NCOL]), ("start", [P, NCOL])):
                k[name] = early.enter_context(nc.sbuf_tensor(name + "2", shape, F32))
            deg = early.enter_context(nc.sbuf_tensor("deg2", [P, NCOL], F32))
            counters(nc, k)
            sort("by_dst", a["dst"], a["src"], deg, keyrow)
            target_scales(nc, k, deg)
        first_norm(nc, k, a["x"], HA)

        by_dst = lists["by_dst"]

        def gather_pass(name, kind, table, scale=None):
            edge_pass(nc, k, name, by_dst, keyrow, kind, table, AGG, scale)

        inv, dinv = k["edge_invdeg"], k["edge_dinv"]
        s = lambda n: (k["s_w"][:, 2 * n, :], k["s_w"][:, 2 * n + 1, :], k["s_b"][n])
        gather_pass("e0", "sum", HA, inv)
        conv_layer(nc, k, "sage0", "sage", AGG, HA, *s(0), h_out=HB)
        gather_pass("e1", "sum", HB, inv)
        conv_layer(nc, k, "sage1", "sage", AGG, HB, *s(1), h_out=HA)
        gather_pass("e2", "sum", HA, inv)
        conv_layer(nc, k, "sage2", "sage", AGG, HA, *s(2), h_out=HB, g_out=GA, x_in=a["x"], x_out=X1, x_real=True)
        gather_pass("e3", "sum", GA, dinv)
        conv_layer(nc, k, "gcn0", "gcn", AGG, HB, k["g_w"][:, 0, :], k["g_w"][:, 3, :], k["g_b"][0],
                   self_bias=k["g_b"][3], h_out=HA, g_out=GA)
        gather_pass("e4", "sum", GA, dinv)
        conv_layer(nc, k, "gcn1", "gcn", AGG, HA, k["g_w"][:, 1, :], None, k["g_b"][1], h_out=HB, g_out=GA)
        gather_pass("e5", "sum", GA, dinv)
        conv_layer(nc, k, "gcn2", "gcn", AGG, HB, k["g_w"][:, 2, :], None, k["g_b"][2], h_out=HA, x_in=X1,
                   x_out=X2)
        mlp_block(nc, k, HA, AGG2, X2, X1, HB)
        project_qkv(nc, k, HB)
        gather_pass("e6", "attention", k["KV"])
        target_keys.close()
        last_block(nc, k, AGG, HB, X1, out)


def counters(nc, k):
    with Phase(nc, "counters") as ph:
        with nc.Block() as block:
            @block.gpsimd
            def _(pool):
                nc.gpsimd.iota(k["count"][:, :], pattern=[[1, NCOL]], base=0, channel_multiplier=0,
                               allow_small_or_imprecise_dtypes=True)

            @block.vector
            def _(dve):
                nc.vector.memset(k["one"][:, :], 1.0)


_INS = ['x', 'src', 'dst', 'edge_attr_128', 'L0_gnn_Wl1', 'L0_gnn_bl1', 'L0_gnn_Wr1', 'L0_gnn_Wlh', 'L0_gnn_blh',
        'L0_gnn_Wrh', 'L1_gnn_W0', 'L1_gnn_b0', 'L1_gnn_W1', 'L1_gnn_b1', 'L1_gnn_W2', 'L1_gnn_b2', 'L1_gnn_Wr',
        'L1_gnn_br', 'L2_gnn_u', 'L2_gnn_W1', 'L2_gnn_b1', 'L2_gnn_W2', 'L2_gnn_b2', 'L3_gnn_Wq', 'L3_gnn_Wk',
        'L3_gnn_Wv', 'L3_gnn_Wo', 'L3_gnn_bo', 'L3_gnn_ln1_g', 'L3_gnn_ln1_b', 'L3_gnn_W1', 'L3_gnn_b1',
        'L3_gnn_W2', 'L3_gnn_b2', 'L3_gnn_ln2_g', 'L3_gnn_ln2_b']


def kernel(**inputs):
    import numpy as _np
    import concourse.bacc as _bacc
    from concourse import mybir as _mybir
    from concourse.bass_utils import run_bass_kernel_spmd as _run

    nc = _bacc.Bacc("TRN2", target_bir_lowering=False, num_devices=1)
    arrays, args = {}, {}
    for name in _INS:
        v = _np.ascontiguousarray(inputs[name])
        arrays[f"in_{name}_dram"] = v
        args[name] = nc.dram_tensor(f"in_{name}_dram", v.shape, _mybir.dt.from_np(v.dtype), kind="ExternalInput").ap()
    out = nc.dram_tensor("out_0_dram", (N, D), _mybir.dt.float32, kind="ExternalOutput").ap()
    gnn_kernel(nc, args, out)
    r = _run(nc, [arrays], core_ids=[0])
    return r.results[0]["out_0_dram"]
```
